# Optimizing a Trainium2 kernel written in Bass

```python
import numpy as np
import jax
import jax.numpy as jnp

def _softmax(x, axis=-1):
    return jax.nn.softmax(x, axis=axis)

def _gelu(x):
    return jax.nn.gelu(x, approximate=True)

def _silu(x):
    return jax.nn.silu(x)

def _sigmoid(x):
    return jax.nn.sigmoid(x)

def _layernorm(x, axis=-1, eps=1e-05):
    m = jnp.mean(x, axis=axis, keepdims=True)
    v = jnp.var(x, axis=axis, keepdims=True)
    return (x - m) / jnp.sqrt(v + eps)

def _scatter_add(tgt, idx, src, axis=0):
    return tgt.at[idx].add(src)

def _segment_sum(src, seg, n):
    return jax.ops.segment_sum(src, seg, n)
kernel_name = 'mk_sandwich_d1_jaxref_r8_f89b91'

def setup_inputs(seed: int=0):
    np.random.seed(seed)
    _w = jnp.asarray

    def _L0_attn_setup():
        import jax, jax.numpy as jnp
        import numpy as np
        D_MODEL = 128
        N_HEADS = 16
        DH = D_MODEL // N_HEADS
        B, T = (4, 256)
        ROPE_BASE = 10000.0
        EPS = 1e-06

        def _rope(q, k, base=ROPE_BASE):
            half = q.shape[-1] // 2
            freqs = jnp.arange(half, dtype=q.dtype)
            inv_freq = base ** (-freqs / half)
            pos = jnp.arange(q.shape[2], dtype=q.dtype)
            ang = pos[:, None] * inv_freq[None, :]
            c = jnp.cos(ang)[None, None]
            s = jnp.sin(ang)[None, None]

            def rot(x):
                x1 = x[..., :half]
                x2 = x[..., half:2 * half]
                return jnp.concatenate([x1 * c - x2 * s, x1 * s + x2 * c], axis=-1)
            return (rot(q), rot(k))

        def _phi(x):
            return jax.nn.elu(x) + 1.0

        def _forward(x, Wq, Wk, Wv, Wo):
            Bx, Tx, D = x.shape
            H, dh = (N_HEADS, D // N_HEADS)
            q = (x @ Wq.T).reshape(Bx, Tx, H, dh).transpose(0, 2, 1, 3)
            k = (x @ Wk.T).reshape(Bx, Tx, H, dh).transpose(0, 2, 1, 3)
            v = (x @ Wv.T).reshape(Bx, Tx, H, dh).transpose(0, 2, 1, 3)
            q, k = _rope(q, k)
            q = _phi(q)
            k = _phi(k)
            qT = q.transpose(2, 0, 1, 3)
            kT = k.transpose(2, 0, 1, 3)
            vT = v.transpose(2, 0, 1, 3)

            def step(carry, qkv):
                K_sum, KV = carry
                q_t, k_t, v_t = qkv
                K_sum = K_sum + k_t
                KV = KV + k_t[..., :, None] * v_t[..., None, :]
                num = jnp.einsum('bhd,bhde->bhe', q_t, KV)
                den = jnp.maximum(jnp.einsum('bhd,bhd->bh', q_t, K_sum), EPS)
                return ((K_sum, KV), num / den[..., None])
            init = (jnp.zeros((Bx, H, dh), x.dtype), jnp.zeros((Bx, H, dh, dh), x.dtype))
            _, Y = jax.lax.scan(step, init, (qT, kT, vT))
            Y = Y.transpose(1, 0, 2, 3).reshape(Bx, Tx, D)
            return Y @ Wo.T
        key = jax.random.key(seed)
        kx, kq, kk, kv, ko = jax.random.split(key, 5)
        scale = 0.02
        return {'x': jax.random.normal(kx, (B, T, D_MODEL), jnp.float32), 'Wq': jax.random.normal(kq, (D_MODEL, D_MODEL), jnp.float32) * scale, 'Wk': jax.random.normal(kk, (D_MODEL, D_MODEL), jnp.float32) * scale, 'Wv': jax.random.normal(kv, (D_MODEL, D_MODEL), jnp.float32) * scale, 'Wo': jax.random.normal(ko, (D_MODEL, D_MODEL), jnp.float32) * scale}
    _L0_attn_in = _L0_attn_setup()

    def _L0_ffn_setup():
        import jax, jax.numpy as jnp
        import numpy as np
        DIM = 128
        DEPTH = 2
        HEADS = 8
        DIM_HEAD = 64
        WINDOW = 64
        INNER = HEADS * DIM_HEAD
        HID = int(DIM * 4 * 2 / 3)
        B, N = (2, 1024)
        QK_SCALE = 8.0

        def shift_token(t):
            t1, t2 = jnp.split(t, 2, axis=-1)
            t2 = jnp.pad(t2, ((0, 0), (1, 0), (0, 0)))[:, :-1]
            return jnp.concatenate([t1, t2], axis=-1)

        def l2norm(t):
            return t / jnp.clip(jnp.linalg.norm(t, axis=-1, keepdims=True), 1e-12)

        def rotate_half(x):
            x1, x2 = jnp.split(x, 2, axis=-1)
            return jnp.concatenate([-x2, x1], axis=-1)

        def rotary_xpos(q, k):
            n = q.shape[-2]
            half_idx = jnp.arange(0, DIM_HEAD, 2, dtype=jnp.float32)
            inv_freq = 1.0 / 10000.0 ** (half_idx / DIM_HEAD)
            t = jnp.arange(n, dtype=jnp.float32)
            freqs = t[:, None] * inv_freq[None, :]
            freqs = jnp.concatenate([freqs, freqs], axis=-1)
            base = (half_idx + 0.4 * DIM_HEAD) / (1.4 * DIM_HEAD)
            power = (t - n // 2) / float(WINDOW // 2)
            scale = base[None, :] ** power[:, None]
            scale = jnp.concatenate([scale, scale], axis=-1)
            cos, sin = (jnp.cos(freqs), jnp.sin(freqs))
            q = q * cos * scale + rotate_half(q) * sin * scale
            k = k * cos / scale + rotate_half(k) * sin / scale
            return (q, k)

        def local_attention(q, k, v):
            b, h, n, d = q.shape
            w = n // WINDOW
            bq = q.reshape(b, h, w, WINDOW, d) * QK_SCALE
            bk = k.reshape(b, h, w, WINDOW, d)
            bv = v.reshape(b, h, w, WINDOW, d)

            def look_around(t):
                p = jnp.pad(t, ((0, 0), (0, 0), (1, 0), (0, 0), (0, 0)))
                return jnp.concatenate([p[:, :, :w], p[:, :, 1:]], axis=3)
            bk, bv = (look_around(bk), look_around(bv))
            bt = jnp.arange(n).reshape(w, WINDOW)
            btp = jnp.pad(bt, ((1, 0), (0, 0)), constant_values=-1)
            btk = jnp.concatenate([btp[:w], btp[1:]], axis=1)
            sim = jnp.einsum('bhwid,bhwjd->bhwij', bq, bk)
            i = bt[:, :, None]
            j = btk[:, None, :]
            mask = (i < j) | (i > j + WINDOW) | (j == -1)
            sim = jnp.where(mask, -jnp.finfo(sim.dtype).max, sim)
            attn = jax.nn.softmax(sim, axis=-1)
            out = jnp.einsum('bhwij,bhwjd->bhwid', attn, bv)
            return out.reshape(b, h, n, d)

        def _layer(x, wqkv, qs, ksc, wo, lg, lb, w1, b1, w2, b2):
            b, n, _ = x.shape
            h = shift_token(x)
            qkv = h @ wqkv
            q, k, v = jnp.split(qkv, 3, axis=-1)
            to_heads = lambda t: t.reshape(b, n, HEADS, DIM_HEAD).transpose(0, 2, 1, 3)
            q, k, v = (to_heads(q), to_heads(k), to_heads(v))
            q = l2norm(q) * qs
            k = l2norm(k) * ksc
            q, k = rotary_xpos(q, k)
            o = local_attention(q, k, v)
            o = o.transpose(0, 2, 1, 3).reshape(b, n, INNER)
            x = x + o @ wo
            h = shift_token(x)
            mu = h.mean(-1, keepdims=True)
            var = h.var(-1, keepdims=True)
            h = (h - mu) / jnp.sqrt(var + 1e-05) * lg + lb
            h = h @ w1 + b1
            a, g = jnp.split(h, 2, axis=-1)
            h = a * jax.nn.gelu(g, approximate=False)
            x = x + h @ w2 + b2
            return x
        key = jax.random.key(seed)
        ks = jax.random.split(key, 6)
        return {'x': jax.random.normal(ks[0], (B, N, DIM), jnp.float32), 'wqkv': jax.random.normal(ks[1], (DEPTH, DIM, 3 * INNER), jnp.float32) * 0.02, 'q_scale': jnp.ones((DEPTH, DIM_HEAD), jnp.float32), 'k_scale': jnp.ones((DEPTH, DIM_HEAD), jnp.float32), 'wo': jax.random.normal(ks[2], (DEPTH, INNER, DIM), jnp.float32) * 0.02, 'ln_g': jnp.ones((DEPTH, DIM), jnp.float32), 'ln_b': jnp.zeros((DEPTH, DIM), jnp.float32), 'w1': jax.random.normal(ks[3], (DEPTH, DIM, 2 * HID), jnp.float32) * 0.02, 'b1': jnp.zeros((DEPTH, 2 * HID), jnp.float32), 'w2': jax.random.normal(ks[4], (DEPTH, HID, DIM), jnp.float32) * 0.02, 'b2': jnp.zeros((DEPTH, DIM), jnp.float32)}
    _L0_ffn_in = _L0_ffn_setup()
    _d = {'L0_attn_x': _L0_attn_in['x'], 'L0_attn_Wq': _L0_attn_in['Wq'], 'L0_attn_Wk': _L0_attn_in['Wk'], 'L0_attn_Wv': _L0_attn_in['Wv'], 'L0_attn_Wo': _L0_attn_in['Wo'], 'L0_ffn_wqkv': _L0_ffn_in['wqkv'], 'L0_ffn_q_scale': _L0_ffn_in['q_scale'], 'L0_ffn_k_scale': _L0_ffn_in['k_scale'], 'L0_ffn_wo': _L0_ffn_in['wo'], 'L0_ffn_ln_g': _L0_ffn_in['ln_g'], 'L0_ffn_ln_b': _L0_ffn_in['ln_b'], 'L0_ffn_w1': _L0_ffn_in['w1'], 'L0_ffn_b1': _L0_ffn_in['b1'], 'L0_ffn_w2': _L0_ffn_in['w2'], 'L0_ffn_b2': _L0_ffn_in['b2']}
    _x0 = _d['L0_attn_x']
    _d['L0_attn_x'] = jax.random.normal(jax.random.fold_in(jax.random.key(seed), 1), (16, 512, 128), dtype=_x0.dtype)
    del _x0
    return _d

def reference(L0_attn_x, L0_attn_Wq, L0_attn_Wk, L0_attn_Wv, L0_attn_Wo, L0_ffn_wqkv, L0_ffn_q_scale, L0_ffn_k_scale, L0_ffn_wo, L0_ffn_ln_g, L0_ffn_ln_b, L0_ffn_w1, L0_ffn_b1, L0_ffn_w2, L0_ffn_b2):

    def _L0_attn_ref(x, Wq, Wk, Wv, Wo):
        import jax, jax.numpy as jnp
        import numpy as np
        D_MODEL = 128
        N_HEADS = 16
        DH = D_MODEL // N_HEADS
        B, T = (4, 256)
        ROPE_BASE = 10000.0
        EPS = 1e-06

        def _rope(q, k, base=ROPE_BASE):
            half = q.shape[-1] // 2
            freqs = jnp.arange(half, dtype=q.dtype)
            inv_freq = base ** (-freqs / half)
            pos = jnp.arange(q.shape[2], dtype=q.dtype)
            ang = pos[:, None] * inv_freq[None, :]
            c = jnp.cos(ang)[None, None]
            s = jnp.sin(ang)[None, None]

            def rot(x):
                x1 = x[..., :half]
                x2 = x[..., half:2 * half]
                return jnp.concatenate([x1 * c - x2 * s, x1 * s + x2 * c], axis=-1)
            return (rot(q), rot(k))

        def _phi(x):
            return jax.nn.elu(x) + 1.0

        def _forward(x, Wq, Wk, Wv, Wo):
            Bx, Tx, D = x.shape
            H, dh = (N_HEADS, D // N_HEADS)
            q = (x @ Wq.T).reshape(Bx, Tx, H, dh).transpose(0, 2, 1, 3)
            k = (x @ Wk.T).reshape(Bx, Tx, H, dh).transpose(0, 2, 1, 3)
            v = (x @ Wv.T).reshape(Bx, Tx, H, dh).transpose(0, 2, 1, 3)
            q, k = _rope(q, k)
            q = _phi(q)
            k = _phi(k)
            qT = q.transpose(2, 0, 1, 3)
            kT = k.transpose(2, 0, 1, 3)
            vT = v.transpose(2, 0, 1, 3)

            def step(carry, qkv):
                K_sum, KV = carry
                q_t, k_t, v_t = qkv
                K_sum = K_sum + k_t
                KV = KV + k_t[..., :, None] * v_t[..., None, :]
                num = jnp.einsum('bhd,bhde->bhe', q_t, KV)
                den = jnp.maximum(jnp.einsum('bhd,bhd->bh', q_t, K_sum), EPS)
                return ((K_sum, KV), num / den[..., None])
            init = (jnp.zeros((Bx, H, dh), x.dtype), jnp.zeros((Bx, H, dh, dh), x.dtype))
            _, Y = jax.lax.scan(step, init, (qT, kT, vT))
            Y = Y.transpose(1, 0, 2, 3).reshape(Bx, Tx, D)
            return Y @ Wo.T
        return _forward(x, Wq, Wk, Wv, Wo)

    def _L0_ffn_ref(x, wqkv, q_scale, k_scale, wo, ln_g, ln_b, w1, b1, w2, b2):
        import jax, jax.numpy as jnp
        import numpy as np
        DIM = 128
        DEPTH = 2
        HEADS = 8
        DIM_HEAD = 64
        WINDOW = 64
        INNER = HEADS * DIM_HEAD
        HID = int(DIM * 4 * 2 / 3)
        B, N = (2, 1024)
        QK_SCALE = 8.0

        def shift_token(t):
            t1, t2 = jnp.split(t, 2, axis=-1)
            t2 = jnp.pad(t2, ((0, 0), (1, 0), (0, 0)))[:, :-1]
            return jnp.concatenate([t1, t2], axis=-1)

        def l2norm(t):
            return t / jnp.clip(jnp.linalg.norm(t, axis=-1, keepdims=True), 1e-12)

        def rotate_half(x):
            x1, x2 = jnp.split(x, 2, axis=-1)
            return jnp.concatenate([-x2, x1], axis=-1)

        def rotary_xpos(q, k):
            n = q.shape[-2]
            half_idx = jnp.arange(0, DIM_HEAD, 2, dtype=jnp.float32)
            inv_freq = 1.0 / 10000.0 ** (half_idx / DIM_HEAD)
            t = jnp.arange(n, dtype=jnp.float32)
            freqs = t[:, None] * inv_freq[None, :]
            freqs = jnp.concatenate([freqs, freqs], axis=-1)
            base = (half_idx + 0.4 * DIM_HEAD) / (1.4 * DIM_HEAD)
            power = (t - n // 2) / float(WINDOW // 2)
            scale = base[None, :] ** power[:, None]
            scale = jnp.concatenate([scale, scale], axis=-1)
            cos, sin = (jnp.cos(freqs), jnp.sin(freqs))
            q = q * cos * scale + rotate_half(q) * sin * scale
            k = k * cos / scale + rotate_half(k) * sin / scale
            return (q, k)

        def local_attention(q, k, v):
            b, h, n, d = q.shape
            w = n // WINDOW
            bq = q.reshape(b, h, w, WINDOW, d) * QK_SCALE
            bk = k.reshape(b, h, w, WINDOW, d)
            bv = v.reshape(b, h, w, WINDOW, d)

            def look_around(t):
                p = jnp.pad(t, ((0, 0), (0, 0), (1, 0), (0, 0), (0, 0)))
                return jnp.concatenate([p[:, :, :w], p[:, :, 1:]], axis=3)
            bk, bv = (look_around(bk), look_around(bv))
            bt = jnp.arange(n).reshape(w, WINDOW)
            btp = jnp.pad(bt, ((1, 0), (0, 0)), constant_values=-1)
            btk = jnp.concatenate([btp[:w], btp[1:]], axis=1)
            sim = jnp.einsum('bhwid,bhwjd->bhwij', bq, bk)
            i = bt[:, :, None]
            j = btk[:, None, :]
            mask = (i < j) | (i > j + WINDOW) | (j == -1)
            sim = jnp.where(mask, -jnp.finfo(sim.dtype).max, sim)
            attn = jax.nn.softmax(sim, axis=-1)
            out = jnp.einsum('bhwij,bhwjd->bhwid', attn, bv)
            return out.reshape(b, h, n, d)

        def _layer(x, wqkv, qs, ksc, wo, lg, lb, w1, b1, w2, b2):
            b, n, _ = x.shape
            h = shift_token(x)
            qkv = h @ wqkv
            q, k, v = jnp.split(qkv, 3, axis=-1)
            to_heads = lambda t: t.reshape(b, n, HEADS, DIM_HEAD).transpose(0, 2, 1, 3)
            q, k, v = (to_heads(q), to_heads(k), to_heads(v))
            q = l2norm(q) * qs
            k = l2norm(k) * ksc
            q, k = rotary_xpos(q, k)
            o = local_attention(q, k, v)
            o = o.transpose(0, 2, 1, 3).reshape(b, n, INNER)
            x = x + o @ wo
            h = shift_token(x)
            mu = h.mean(-1, keepdims=True)
            var = h.var(-1, keepdims=True)
            h = (h - mu) / jnp.sqrt(var + 1e-05) * lg + lb
            h = h @ w1 + b1
            a, g = jnp.split(h, 2, axis=-1)
            h = a * jax.nn.gelu(g, approximate=False)
            x = x + h @ w2 + b2
            return x
        for l in range(DEPTH):
            x = _layer(x, wqkv[l], q_scale[l], k_scale[l], wo[l], ln_g[l], ln_b[l], w1[l], b1[l], w2[l], b2[l])
        return x
    x = L0_attn_x
    x = x + _layernorm(_L0_attn_ref(_layernorm(x, axis=-1), L0_attn_Wq, L0_attn_Wk, L0_attn_Wv, L0_attn_Wo), axis=-1)
    x = x + _layernorm(_L0_ffn_ref(_layernorm(x, axis=-1), L0_ffn_wqkv, L0_ffn_q_scale, L0_ffn_k_scale, L0_ffn_wo, L0_ffn_ln_g, L0_ffn_ln_b, L0_ffn_w1, L0_ffn_b1, L0_ffn_w2, L0_ffn_b2), axis=-1)
    return x

_drawn_inputs = setup_inputs


def setup_inputs(seed=0):
    import zlib

    import numpy as np

    out = dict(_drawn_inputs(seed))
    spreads = {'L0_ffn_q_scale': (1.0, 0.6),
     'L0_ffn_k_scale': (1.0, 0.6),
     'L0_ffn_ln_g': (1.0, 0.6),
     'L0_ffn_ln_b': (0.0, 0.8),
     'L0_ffn_b1': (0.0, 0.8),
     'L0_ffn_b2': (0.0, 0.8)}
    factors = {'L0_attn_Wq': 5.178, 'L0_ffn_w1': 7.072, 'L0_ffn_w2': 6.938}
    for name, (base, spread) in spreads.items():
        noise = np.random.default_rng([zlib.crc32(name.encode()), seed]).standard_normal(out[name].shape)
        drawn = base * np.exp(spread * noise) if base else spread * noise
        out[name] = jnp.asarray(drawn.astype(out[name].dtype))
    for name, factor in factors.items():
        out[name] = (out[name] * factor).astype(out[name].dtype)
    return out
```

```python
from contextlib import ExitStack

import numpy as np

import concourse.bass as bass
from concourse import mybir

B, T, D = 16, 512, 128
P = 128
NT = T // P
STREAMS = 2
ROUNDS = B // STREAMS
LA_HEADS, LA_DH = 16, 8
GROUPS, SLOTS = 4, 4
DEPTH, HEADS, DH, WIN = 2, 8, 64, 64
INNER = HEADS * DH
PAIRS = HEADS // 2
HID = int(D * 4 * 2 / 3)
HID_CHUNKS = [(0, 128), (128, 128), (256, HID - 256)]
UNITS = NT * 2
QK_SCALE = 8.0
KPAD = 576
ODD = 256
VW = DH + 1
MASKED = -float(2.0 ** 100)
LN_EPS, DEN_EPS, NORM_EPS = 1e-5, 1e-6, 1e-12
BANKS = 8

CONST_COLS = {}
SETUP_ONLY = ("mask_first", "mask_later", "q_cos", "q_sin", "k_cos", "k_sin")


def _constants():
    f = np.float32
    p = np.arange(P)
    parts = []

    def put(name, a):
        a = np.ascontiguousarray(np.asarray(a, f).reshape(P, -1))
        CONST_COLS[name] = (sum(x.shape[1] for x in parts), a.shape[1])
        parts.append(a)

    put("ident", np.eye(P))
    put("shift", np.eye(P, k=1))
    wrap = np.zeros((P, P), f)
    wrap[P - 1, 0] = 1
    put("wrap", wrap)
    put("causal", (p[:, None] <= p[None, :]))
    put("block", np.tile(p[:, None] // LA_DH == p[None, :] // LA_DH, (1, 2)))
    put("slot", (p[:, None] // LA_DH) % SLOTS == np.arange(SLOTS)[None, :])
    put("ones_slot", np.tile((np.arange(SLOTS)[:, None] == (np.arange(32) // LA_DH)[None, :])[None], (P, 1, 1)))
    put("ones", np.ones((P, 1)))
    put("zeros", np.zeros((P, 1)))
    half = LA_DH // 2
    inv = (f(10000.0) ** (-np.arange(half, dtype=f) / f(half))).astype(f)
    ang = (np.arange(T, dtype=f)[:, None] * inv[None, :]).astype(f)
    c, s = np.cos(ang), np.sin(ang)
    rows = lambda a: a.reshape(NT, P, -1).transpose(1, 0, 2)
    put("la_cos", rows(np.concatenate([c, c], 1)))
    put("la_sin", rows(np.concatenate([-s, s], 1)))
    q, k = np.arange(WIN)[:, None], np.arange(WIN)[None, :]
    own, before = np.where(k <= q, 0, MASKED), np.where(k >= q, 0, MASKED)
    later = np.concatenate([np.concatenate([own, before], 1), np.concatenate([before, own], 1)], 0)
    first = later.copy()
    first[:WIN, WIN:] = MASKED
    put("mask_first", np.tile(first, (1, 4)))
    put("mask_later", np.tile(later, (1, 4)))
    idx = np.arange(0, DH, 2, dtype=f)
    inv = (f(1.0) / f(10000.0) ** (idx / f(DH))).astype(f)
    t = np.arange(T, dtype=f)
    ang = (t[:, None] * inv[None, :]).astype(f)
    base = ((idx + f(0.4 * DH)) / f(1.4 * DH)).astype(f)
    scale = (base[None, :] ** ((t - T // 2) / f(WIN // 2))[:, None]).astype(f)
    c, s = np.cos(ang), np.sin(ang)
    put("q_cos", rows(np.concatenate([c * scale, c * scale], 1)))
    put("q_sin", rows(np.concatenate([-s * scale, s * scale], 1)))
    put("k_cos", rows(np.concatenate([c / scale, c / scale], 1)))
    put("k_sin", rows(np.concatenate([-s / scale, s / scale], 1)))
    return np.concatenate(parts, 1)


CONSTANTS = _constants()
NCONST = CONST_COLS["mask_first"][0]
NSETUP = CONSTANTS.shape[1] - NCONST


class Step:

    def __init__(self, kind, s, l=0, j=0, n=0):
        self.kind, self.s, self.l, self.j, self.n = kind, s, l, j, n

    def moved(self, by):
        return Step(self.kind, self.s, self.l, self.j, self.n + by)


def linear_steps(s, n):
    out = [Step("ln_in", s, n=n), Step("yt", s, n=n)]
    for t in range(NT + 3):
        for lag, kind in ((3, "ao"), (2, "as"), (1, "at"), (0, "aqkv")):
            if 0 <= t - lag < NT:
                out.append(Step(kind, s, 0, t - lag, n))
    out += [Step("awo", s, n=n), Step("ln_attn", s, n=n), Step("ln_mid", s, n=n)]
    return out + qkv_steps(s, 0, n)


def qkv_steps(s, l, n=0):
    out = [Step("h", s, l, 0, n)]
    for t in range(NT + 2):
        for lag, kind in ((2, "qkt"), (0, "qkv")):
            if 0 <= t - lag < NT:
                out.append(Step(kind, s, l, t - lag, n))
    return out


def attention_steps(s, l):
    out = []
    for t in range(UNITS + 6):
        for lag, kind in ((5, "wo"), (4, "ot")):
            if 0 <= t - lag < UNITS and (t - lag) % 2:
                out.append(Step(kind, s, l, (t - lag) // 2))
        for lag, kind in ((3, "o"), (2, "pt"), (0, "s")):
            if 0 <= t - lag < UNITS:
                out.append(Step(kind, s, l, t - lag))
    return out


def ffn_steps(s, l):
    return [Step(k, s, l) for k in ("sh", "ln_ffn", "h2t", "w1", "w2")]


COST = {"yt": 1, "aqkv": 1, "at": 1, "as": 2, "ao": 2.5, "awo": 1, "h": 1, "qkv": 2.6, "qkt": 1, "s": 1.2, "pt": 0.5,
        "o": 1.3, "ot": 0.5, "wo": 1, "sh": 1, "h2t": 0.5, "w1": 5, "w2": 2.6, "ln_in": 1, "ln_attn": 1, "ln_mid": 1,
        "ln_ffn": 1, "ln_out": 1}


def side_by_side(a, b):
    placed = []
    for lane, steps in enumerate((a, b)):
        whole = sum(COST[x.kind] for x in steps)
        at = 0.0
        for x in steps:
            placed.append((at / whole, lane, len(placed), x))
            at += COST[x.kind]
    return [x[3] for x in sorted(placed, key=lambda x: x[:3])]


def round_steps(with_next):
    ends = [ffn_steps(s, 1) + [Step("ln_out", s)] for s in (0, 1)]
    return (side_by_side(attention_steps(0, 0), linear_steps(1, 0))
            + side_by_side(ffn_steps(0, 0) + qkv_steps(0, 1), attention_steps(1, 0))
            + side_by_side(attention_steps(0, 1), ffn_steps(1, 0) + qkv_steps(1, 1))
            + side_by_side(ends[0], attention_steps(1, 1))
            + side_by_side(ends[1], linear_steps(0, 1) if with_next else []))


LN_ORDER = {"ln_in": 0, "ln_attn": 1, "ln_mid": 2, "ln_ffn": 3, "ln_out": 5}


def order_of(step):
    if step.kind in LN_ORDER:
        return LN_ORDER[step.kind] + (step.l if step.kind == "ln_ffn" else 0)
    return step.l * tiles_of(step.kind) + step.j


def tiles_of(kind):
    if kind in ("s", "pt", "o"):
        return UNITS
    if kind in ("qkv", "qkt", "ot", "wo", "aqkv", "at", "as", "ao"):
        return NT
    return 1


def steps_of(kind):
    if kind in LN_ORDER:
        return 6
    return tiles_of(kind) * (DEPTH if kind in ("h", "qkv", "qkt", "s", "pt", "o", "ot", "wo", "sh", "h2t", "w1", "w2") else 1)


class Signal:

    def __init__(self, nc, ctx, name, kind, incs=1, per_inc=1, steps=None):
        self.steps = steps_of(kind) if steps is None else steps
        self.incs, self.per_inc = incs, per_inc
        self.sems = [ctx.enter_context(nc.semaphore(f"{name}_{s}")) for s in range(STREAMS)]

    def start(self):
        return self.steps * self.incs * self.per_inc

    def of(self, step):
        return self.sems[step.s]

    def at(self, i, step, k=None, back=0, order=None):
        k = self.incs if k is None else k
        order = order_of(step) if order is None else order
        fixed = (((step.n + 1) * self.steps + order - back) * self.incs + k) * self.per_inc
        return self.sems[step.s], i.times(self.start()) + fixed


class Round:

    def __init__(self, eng, i):
        self.eng, self.i, self.kept = eng, i, {}

    def times(self, by):
        if isinstance(self.i, int):
            return self.i * by
        if by not in self.kept:
            self.kept[by] = self.eng.snap(self.i * by)
        return self.kept[by]


def build(nc, x, wq, wk, wv, wo_la, wqkv, q_scale, k_scale, wo, ln_g, ln_b, w1, b1, w2, b2, consts, out):
    f32, bf16 = mybir.dt.float32, mybir.dt.bfloat16
    ALU, ACT, AX = mybir.AluOpType, mybir.ActivationFunctionType, mybir.AxisListType
    ctx = ExitStack()
    nc.disable_value_cache = True

    with ctx:
        def sb(name, shape, dt=f32):
            return ctx.enter_context(nc.sbuf_tensor(name, shape, dt))

        const = sb("const", [P, NCONST])
        setup_const = None

        def cst(name):
            at, n = CONST_COLS[name]
            return setup_const[:, at - NCONST:at - NCONST + n] if name in SETUP_ONLY else const[:, at:at + n]

        ident = cst("ident")
        ident_h = sb("ident_h", [P, P], bf16)
        mask_h = sb("mask_h", [P, 2, 4 * P], bf16)
        w_la = sb("w_la", [P, 3 * D])
        wo_la_t = sb("wo_la_t", [P, D])
        wqkv_sb = sb("wqkv_sb", [P, DEPTH, 3 * INNER])
        wo_sb = sb("wo_sb", [P, DEPTH, PAIRS, D])
        w1_sb = sb("w1_sb", [P, DEPTH, 2 * HID])
        w2_sb = sb("w2_sb", [P, DEPTH, 3, D])
        b2_rows = sb("b2_rows", [P, DEPTH, D])
        b1_cols = sb("b1_cols", [P, DEPTH, 2, 3])
        ln_cols = sb("ln_cols", [P, DEPTH, 2])
        rope = sb("rope", [P, DEPTH, 4, NT * DH])
        qk_scale = sb("qk_scale", [P, DEPTH, 2, DH])
        minus_half = sb("minus_half", [P, 16])

        x_io = [sb(f"x_io{s}", [P, NT, D]) for s in range(STREAMS)]
        x_res = [sb(f"x_res{s}", [P, NT, D]) for s in range(STREAMS)]
        q_cols = [sb(f"q_cols{s}", [P, PAIRS, T]) for s in range(STREAMS)]
        k_cols = [sb(f"k_cols{s}", [P, PAIRS, 2, KPAD]) for s in range(STREAMS)]
        v_rows = [sb(f"v_rows{s}", [P, NT, HEADS, VW]) for s in range(STREAMS)]
        v_even = [sb(f"v_even{s}", [P, NT, HEADS, VW]) for s in range(STREAMS)]
        qk_rnorm = [sb(f"qk_rnorm{s}", [P, NT, 2 * HEADS]) for s in range(STREAMS)]
        qk_ss = [sb(f"qk_ss{s}", [P, NT, 2 * HEADS]) for s in range(STREAMS)]
        ln_stats = [sb(f"ln_stats{s}", [P, 6, NT, 6]) for s in range(STREAMS)]
        ln_mv = [sb(f"ln_mv{s}", [P, 6, NT, 2]) for s in range(STREAMS)]
        ln_var = [sb(f"ln_var{s}", [P, 6, NT]) for s in range(STREAMS)]
        ln_rstd = [sb(f"ln_rstd{s}", [P, 6, NT]) for s in range(STREAMS)]
        ln_held = [sb(f"ln_held{s}", [P, 6]) for s in range(STREAMS)]
        la_state = [sb(f"la_state{s}", [P, 2 * D]) for s in range(STREAMS)]

        y_cols = sb("y_cols", [P, T])
        la_ta = sb("la_ta", [P, 2, 2 * D])
        la_tb = sb("la_tb", [P, 2, 2 * D])
        la_r = sb("la_r", [P, 2, 2 * D])
        la_phi = sb("la_phi", [P, NT, 2 * D])
        la_v = sb("la_v", [P, NT, D])
        la_vslot = sb("la_vslot", [P, 2, LA_HEADS, 32])
        la_qk_cols = sb("la_qk_cols", [P, 2, 2 * P])
        la_den = sb("la_den", [P, P])
        la_tmp = sb("la_tmp", [P, 2 * D])
        room = sb("room", [P, 5120])
        la_qexp = room[:, 0:1024].rearrange("p (a s q) -> p a s q", a=2, s=SLOTS)
        la_sm = room[:, 1024:5120].rearrange("p (a g s q) -> p a g s q", a=2, g=GROUPS, s=SLOTS)
        y_rows = room[:, 1024:1536].rearrange("p (j d) -> p j d", j=NT)
        qk_sq = room[:, 0:1024]
        qk_t = room[:, 1024:5120].rearrange("p (a w c n) -> p a w c n", a=2, w=2, c=2)
        h_cols = sb("h_cols", [P, T])
        probs = sb("probs", [P, 2, 4 * P])
        probs_t = sb("probs_t", [P, 2, 4 * P])
        s_max = sb("s_max", [P, 2, 4])
        s_bias = sb("s_bias", [P, 2, 4])
        o_rden = sb("o_rden", [P, 2, 4])
        o_rows = sb("o_rows", [P, INNER])
        o_cols = sb("o_cols", [P, INNER])
        h2_rows = sb("h2_rows", [P, NT, D])
        h2_cols = sb("h2_cols", [P, T])
        hidden = sb("hidden", [P, 3, T])

        def k_windows(of, ahead, first):
            ap = of[..., first:first + WIN]
            return bass.AP(tensor=ap.tensor, offset=ap.offset, ap=[*ap.ap[:-1], [ODD + ahead, 2], list(ap.ap[-1])])

        bank = [ctx.enter_context(nc.psum_tensor(f"bank{b}", [P, 512], f32)) for b in range(BANKS)]

        def signal(name, kind, incs=1, per_inc=1, steps=None):
            return Signal(nc, ctx, name, kind, incs, per_inc, steps)

        pe_yt = signal("pe_yt", "yt")
        pe_aqkv = signal("pe_aqkv", "aqkv")
        pe_at = signal("pe_at", "at")
        pe_as = signal("pe_as", "as", GROUPS)
        pe_ao = signal("pe_ao", "ao")
        pe_awo = signal("pe_awo", "awo")
        pe_h = signal("pe_h", "h")
        pe_qkv = signal("pe_qkv", "qkv", 3)
        pe_qkt = signal("pe_qkt", "qkt", 2)
        pe_s = signal("pe_s", "s")
        pe_pt = signal("pe_pt", "pt")
        pe_o = signal("pe_o", "o")
        pe_ot = signal("pe_ot", "ot")
        pe_wo = signal("pe_wo", "wo")
        pe_sh = signal("pe_sh", "sh")
        pe_h2t = signal("pe_h2t", "h2t")
        pe_w1 = signal("pe_w1", "w1", 6)
        pe_w2 = signal("pe_w2", "w2")
        act_yt = signal("act_yt", "yt")
        act_av = signal("act_av", "aqkv")
        act_slots = signal("act_slots", "as")
        act_aexp = signal("act_aexp", "aqkv")
        act_at = signal("act_at", "at")
        act_h = signal("act_h", "h", 2)
        act_qkv = signal("act_qkv", "qkv", 3)
        act_q = signal("act_q", "qkt")
        act_p = signal("act_p", "s", 4)
        act_pt = signal("act_pt", "pt")
        act_ot = signal("act_ot", "ot")
        act_h2x = signal("act_h2x", "sh")
        act_h2t = signal("act_h2t", "h2t")
        act_gelu = signal("act_gelu", "w1", 3)
        dve_ln = signal("dve_ln", "ln_in", 4 + 4 + 1 + 4)
        dve_arope = signal("dve_arope", "aqkv", 2)
        dve_aphi = signal("dve_aphi", "aqkv", 2)
        dve_qexp = signal("dve_qexp", "at")
        dve_sm = signal("dve_sm", "as", GROUPS)
        dve_ao = signal("dve_ao", "ao", 3)
        dve_state = signal("dve_state", "ao", 2, steps=NT - 1)
        dve_xmid = signal("dve_xmid", "ln_attn", steps=1)
        dve_rope = signal("dve_rope", "qkv", 6)
        dve_k = signal("dve_k", "qkt", 2)
        dve_max = signal("dve_max", "s", 2)
        dve_on = signal("dve_on", "o", 2)
        dve_wo = signal("dve_wo", "wo")
        dve_h2 = signal("dve_h2", "sh")
        dve_u = signal("dve_u", "w1", 3)
        dve_w2 = signal("dve_w2", "w2")
        dve_out = signal("dve_out", "ln_out", steps=1)
        pool_rstd = signal("pool_rstd", "ln_in")
        pool_ar = signal("pool_ar", "aqkv")
        pool_rnorm = signal("pool_rnorm", "qkv")
        pool_qk = signal("pool_qk", "qkv", 3)
        pool_ve = signal("pool_ve", "qkv", 2)
        pool_b2 = signal("pool_b2", "sh")
        x_loaded = signal("x_loaded", "ln_in", 1, 16, steps=1)
        out_stored = signal("out_stored", "ln_out", 1, 16, steps=1)
        every = [v for v in list(locals().values()) if isinstance(v, Signal)]

        RELEASED = {
            "yt": [(act_yt, 1)], "aqkv": [(dve_arope, 2)], "at": [(act_at, 1)],
            "as": [(dve_sm, g + 1) for g in range(GROUPS)], "ao": [(dve_ao, 3)], "awo": [(dve_ln, 13)],
            "h": [(act_h, 2)], "qkv": [(dve_rope, 2), (dve_rope, 4), (act_qkv, 3)],
            "qkt": [(act_q, 1), (dve_k, 2)], "s": [(act_p, 4)], "pt": [(act_pt, 1)], "o": [(dve_on, 2)],
            "ot": [(act_ot, 1)], "wo": [(dve_wo, 1)], "sh": [(dve_h2, 1)], "h2t": [(act_h2t, 1)],
            "w1": [(act_gelu, c + 1) for c in range(3)] + [(dve_u, c + 1) for c in range(3)],
            "w2": [(dve_w2, 1)],
        }

        def plan(steps, users):
            taken, n = [], 0
            users = dict(users)
            for step in steps:
                mine = []
                for sig, k in RELEASED.get(step.kind, []):
                    b = n % BANKS
                    mine.append((b, users.get(b, [])))
                    last = Step("ln_attn", step.s, n=step.n) if step.kind == "awo" else step
                    users[b] = [(sig, k, last)]
                    n += 1
                taken.append(mine)
            return taken, users

        def one_round_on(users):
            return {b: [(sig, k, st.moved(-1)) for sig, k, st in u] for b, u in users.items()}

        first_steps = linear_steps(0, 1)
        body_steps, last_steps = round_steps(True), round_steps(False)
        first_plan, first_users = plan(first_steps, {})
        _, body_users = plan(body_steps, {})
        before = {b: one_round_on(body_users).get(b, []) + one_round_on(first_users).get(b, []) for b in range(BANKS)}
        body_plan, _ = plan(body_steps, before)
        last_plan, _ = plan(last_steps, before)

        def whole_program(eng, run):
            run(Round(eng, -1), first_steps, first_plan)
            with eng.Fori(0, ROUNDS - 1) as i:
                run(Round(eng, i), body_steps, body_plan)
            run(Round(eng, ROUNDS - 1), last_steps, last_plan)

        setup_const = room[:, 4 * D:4 * D + NSETUP]
        loaded = ctx.enter_context(nc.semaphore("weights_loaded"))
        turned = ctx.enter_context(nc.semaphore("weights_turned"))
        setup_dve = ctx.enter_context(nc.semaphore("setup_dve"))
        LOADS = 2 + 4 + DEPTH * (1 + 1 + 1 + 1 + 1 + 1 + 6 + 2 + 2)

        with nc.Block() as block:
            @block.sync
            def _(sp):
                sp.dma_start(const[:, :], consts[:, 0:NCONST]).then_inc(loaded, 16)
                sp.dma_start(setup_const, consts[:, NCONST:NCONST + NSETUP]).then_inc(loaded, 16)
                for n, w in enumerate((wq, wk, wv, wo_la)):
                    sp.dma_start(room[:, n * D:(n + 1) * D], w).then_inc(loaded, 16)
                for l in range(DEPTH):
                    sp.dma_start(wqkv_sb[:, l, :], wqkv[l]).then_inc(loaded, 16)
                    sp.dma_start(wo_sb[:, l, :, :], wo[l].rearrange("(c p) n -> p c n", p=P)).then_inc(loaded, 16)
                    sp.dma_start(w1_sb[:, l, :], w1[l]).then_inc(loaded, 16)
                    sp.dma_start(w2_sb[:, l, 0:2, :], w2[l, 0:256, :].rearrange("(c p) n -> p c n", p=P)).then_inc(loaded, 16)
                    sp.dma_start(w2_sb[0:HID - 256, l, 2, :], w2[l, 256:HID, :]).then_inc(loaded, 16)
                    sp.dma_start(b2_rows[:, l, :], b2[l:l + 1, :].to_broadcast([P, D])).then_inc(loaded, 16)
                    for half in range(2):
                        for c, (at, n) in enumerate(HID_CHUNKS):
                            sp.dma_start(b1_cols[0:n, l, half, c:c + 1],
                                         b1[l, half * HID + at:half * HID + at + n].unsqueeze(1)).then_inc(loaded, 16)
                    sp.dma_start(ln_cols[:, l, 0:1], ln_g[l].unsqueeze(1)).then_inc(loaded, 16)
                    sp.dma_start(ln_cols[:, l, 1:2], ln_b[l].unsqueeze(1)).then_inc(loaded, 16)
                    sp.dma_start(qk_scale[:, l, 0, :], q_scale[l:l + 1, :].to_broadcast([P, DH])).then_inc(loaded, 16)
                    sp.dma_start(qk_scale[:, l, 1, :], k_scale[l:l + 1, :].to_broadcast([P, DH])).then_inc(loaded, 16)
                for sig in every:
                    for sem in sig.sems:
                        sp.sem_inc(sem, sig.start())

            @block.gpsimd
            def _(pool):
                for s in range(STREAMS):
                    pool.memset(k_cols[s][:, :, :, :], 0.0)
                    pool.memset(v_even[s][:, :, :, :], 0.0)
                    pool.memset(v_rows[s][:, :, :, :], 1.0)
                pool.memset(la_vslot[:, :, :, :], 0.0)
                pool.memset(h_cols[:, :], 0.0)
                pool.memset(minus_half[:, :], -0.5)

            @block.tensor
            def _(pe):
                pe.wait_ge(loaded, 16 * LOADS)
                for n in range(4):
                    mm = pe.transpose(bank[0][:, n * D:(n + 1) * D], room[:, n * D:(n + 1) * D], ident)
                mm.then_inc(turned, 1)

            @block.vector
            def _(dve):
                dve.wait_ge(loaded, 16 * LOADS)
                dve.tensor_copy(ident_h[:, :], ident)
                dve.tensor_copy(mask_h[:, 0, :], cst("mask_first"))
                dve.tensor_copy(mask_h[:, 1, :], cst("mask_later"))
                for l in range(DEPTH):
                    for w, (names, by) in enumerate(((("q_cos", "q_sin"), QK_SCALE), (("k_cos", "k_sin"), 1.0))):
                        sc = qk_scale[:, l, w, :].rearrange("p (a b) -> p a b", a=2)
                        for c, name in enumerate(names):
                            scales = sc[:, ::-1, :] if c else sc
                            for j in range(NT):
                                dve.scalar_tensor_tensor(
                                    out=rope[:, l, 2 * w + c, j * DH:(j + 1) * DH].rearrange("p (a b) -> p a b", a=2),
                                    in0=cst(name)[:, j * DH:(j + 1) * DH].rearrange("p (a b) -> p a b", a=2),
                                    scalar=by, in1=scales, op0=ALU.mult, op1=ALU.mult)
                dve.wait_ge(turned, 1)
                dve.tensor_copy(w_la[:, :], bank[0][:, 0:3 * D])
                dve.tensor_copy(wo_la_t[:, :], bank[0][:, 3 * D:4 * D])

        with nc.Block() as block:
            @block.sync
            def _(sp):
                def load(i, s, n):
                    st = Step("ln_in", s, n=n)
                    sp.wait_ge(*out_stored.at(i, st, back=1, order=0))
                    sp.dma_start(x_io[s][:, :, :], x[bass.ds(i.i * STREAMS + n * STREAMS + s, 1), :, :].rearrange(
                        "o (j p) d -> p (o j) d", p=P)).then_inc(x_loaded.of(st), 16)

                def store(i, s):
                    st = Step("ln_out", s)
                    sp.wait_ge(*dve_out.at(i, st, order=0))
                    sp.dma_start(out[bass.ds(i.i * STREAMS + s, 1), :, :].rearrange("o (j p) d -> p (o j) d", p=P),
                                 x_io[s][:, :, :]).then_inc(out_stored.of(st), 16)

                load(Round(sp, -1), 0, 1)
                with sp.Fori(0, ROUNDS - 1) as counter:
                    i = Round(sp, counter)
                    load(i, 1, 0)
                    store(i, 0)
                    load(i, 0, 1)
                    store(i, 1)
                last = Round(sp, ROUNDS - 1)
                load(last, 1, 0)
                store(last, 0)
                store(last, 1)
                for s in range(STREAMS):
                    sp.wait_ge(*out_stored.at(last, Step("ln_out", s), order=0))

            @block.tensor
            def _(pe):
                def take(i, banks, use):
                    b, users = banks[use]
                    for sig, k, st in users:
                        pe.wait_ge(*sig.at(i, st, k, order=0 if sig.steps == 1 else None))
                    return bank[b]

                def yt(i, st, banks):
                    to = take(i, banks, 0)
                    pe.wait_ge(*dve_ln.at(i, Step("ln_in", st.s, n=st.n)))
                    for j in range(NT):
                        mm = pe.transpose(to[:, j * P:(j + 1) * P], y_rows[:, j, :], ident)
                    mm.then_inc(pe_yt.of(st), 1)

                def aqkv(i, st, banks):
                    to = take(i, banks, 0)
                    pe.wait_ge(*act_yt.at(i, Step("yt", st.s, n=st.n)))
                    pe.matmul(to[:, 0:3 * D], y_cols[:, st.j * P:(st.j + 1) * P], w_la[:, :],
                              start=True, stop=True).then_inc(pe_aqkv.of(st), 1)

                def at(i, st, banks):
                    to = take(i, banks, 0)
                    pe.wait_ge(*dve_aphi.at(i, Step("aqkv", st.s, 0, st.j, st.n)))
                    for w in range(2):
                        mm = pe.transpose(to[:, w * P:(w + 1) * P], la_phi[:, st.j, w * D:(w + 1) * D], ident)
                    mm.then_inc(pe_at.of(st), 1)

                def scores_linear(i, st, banks):
                    a = st.j % 2
                    pe.wait_ge(*dve_qexp.at(i, Step("at", st.s, 0, st.j, st.n)))
                    for g in range(GROUPS):
                        to = take(i, banks, g)
                        rows = slice(32 * g, 32 * g + 32)
                        pe.matmul(to[:, :], la_qk_cols[rows, a, P:2 * P],
                                  la_qexp[rows, a, :, :].rearrange("p s q -> p (s q)"),
                                  start=True, stop=True).then_inc(pe_as.of(st), 1)

                def out_linear(i, st, banks):
                    j, a = st.j, st.j % 2
                    to = take(i, banks, 0)
                    pe.wait_ge(*act_av.at(i, Step("aqkv", st.s, 0, j, st.n)))
                    q_tile = la_qk_cols[:, a, 0:P]
                    started = False
                    if j < NT - 1:
                        pe.matmul(to[:, 256:384], la_phi[:, j, D:2 * D], la_v[:, j, :], start=True, stop=True,
                                  skip_group_check=True)
                        pe.matmul(to[:, 384:512], la_phi[:, j, D:2 * D], cst("ones").to_broadcast([P, D]), start=False, stop=True,
                                  skip_group_check=True)
                        started = True
                    if j > 0:
                        pe.wait_ge(*dve_state.at(i, st, order=j - 1))
                        pe.matmul(to[:, 0:P], la_state[st.s][:, 0:D], q_tile, start=not started, stop=False,
                                  skip_group_check=True)
                        pe.matmul(to[:, P:2 * P], la_state[st.s][:, D:2 * D], q_tile, start=False, stop=False,
                                  skip_group_check=True)
                    pe.wait_ge(*act_slots.at(i, Step("as", st.s, 0, j, st.n)))
                    for g in range(GROUPS):
                        pe.wait_ge(*dve_sm.at(i, Step("as", st.s, 0, j, st.n), g + 1))
                        for sl in range(SLOTS):
                            mm = pe.matmul(to[32 * g:32 * g + 32, 0:P], la_vslot[:, a, g * SLOTS + sl, :],
                                           la_sm[:, a, g, sl, :], start=False, stop=(sl == SLOTS - 1), skip_group_check=True)
                            mm = pe.matmul(to[32 * g:32 * g + 32, P:2 * P],
                                           cst("ones_slot")[:, sl * 32:(sl + 1) * 32],
                                           la_sm[:, a, g, sl, :], start=False, stop=(sl == SLOTS - 1),
                                           skip_group_check=True)
                    mm.then_inc(pe_ao.of(st), 1)

                def awo(i, st, banks):
                    to = take(i, banks, 0)
                    for j in range(NT):
                        pe.wait_ge(*dve_ao.at(i, Step("ao", st.s, 0, j, st.n)))
                        mm = pe.matmul(to[:, j * D:(j + 1) * D], y_cols[:, j * P:(j + 1) * P], wo_la_t[:, :],
                                       start=True, stop=True)
                    mm.then_inc(pe_awo.of(st), 1)

                def h(i, st, banks):
                    to = take(i, banks, 0)
                    if st.l == 0:
                        pe.wait_ge(*dve_ln.at(i, Step("ln_mid", st.s, n=st.n)))
                    else:
                        pe.wait_ge(*dve_w2.at(i, Step("w2", st.s, st.l - 1, 0, st.n)))
                    for j in range(NT):
                        mm = pe.transpose(to[:, j * P:(j + 1) * P], x_res[st.s][:, j, :], ident)
                    mm.then_inc(pe_h.of(st), 1)

                def qkv(i, st, banks):
                    pe.wait_ge(*act_h.at(i, Step("h", st.s, st.l, 0, st.n)))
                    for w in range(3):
                        to = take(i, banks, w)
                        pe.matmul(to[:, :], h_cols[:, st.j * P:(st.j + 1) * P],
                                  wqkv_sb[:, st.l, w * INNER:(w + 1) * INNER],
                                  start=True, stop=True).then_inc(pe_qkv.of(st), 1)

                def qkt(i, st, banks):
                    a = st.j % 2
                    qkv_step = Step("qkv", st.s, st.l, st.j, st.n)
                    for w in range(2):
                        to = take(i, banks, w)
                        pe.wait_ge(*pool_qk.at(i, qkv_step, 1 + 2 * w))
                        for c in range(PAIRS):
                            mm = pe.transpose(to[:, c * P:(c + 1) * P], qk_t[:, a, w, 0, c * P:(c + 1) * P], ident)
                        mm.then_inc(pe_qkt.of(st), 1)

                def scores(i, st, banks):
                    j, g = st.j // 2, st.j % 2
                    to = take(i, banks, 0)
                    tile = Step("qkt", st.s, st.l, j, st.n)
                    if g == 0:
                        pe.wait_ge(*act_q.at(i, tile))
                        pe.wait_ge(*dve_k.at(i, tile))
                    pe.matmul(to[:, :], ident_h[:, :], mask_h[:, min(j, 1), :], start=True, stop=False,
                              skip_group_check=True)
                    for c in range(2):
                        pair = 2 * g + c
                        for w in range(2):
                            first = j * WIN
                            keys = k_windows(k_cols[st.s][:, pair, :, :], w * WIN, first)
                            mm = pe.matmul(to[w * WIN:(w + 1) * WIN, c * 256:(c + 1) * 256],
                                           q_cols[st.s][:, pair, j * P + w * WIN:j * P + (w + 1) * WIN], keys,
                                           start=False, stop=True, skip_group_check=True)
                    mm.then_inc(pe_s.of(st), 1)

                def turn_probs(i, st, banks):
                    to = take(i, banks, 0)
                    pe.wait_ge(*act_p.at(i, Step("s", st.s, st.l, st.j, st.n)))
                    for n in range(4):
                        mm = pe.transpose(to[:, n * P:(n + 1) * P], probs[:, st.j % 2, n * P:(n + 1) * P], ident)
                    mm.then_inc(pe_pt.of(st), 1)

                def mix(i, st, banks):
                    j, g = st.j // 2, st.j % 2
                    to = take(i, banks, 0)
                    tile = Step("qkv", st.s, st.l, j, st.n)
                    if g == 0:
                        pe.wait_ge(*act_qkv.at(i, tile, 3))
                        pe.wait_ge(*pool_ve.at(i, tile))
                    pe.wait_ge(*act_pt.at(i, Step("pt", st.s, st.l, st.j, st.n)))
                    for n in range(4):
                        for w in range(2):
                            values = (v_even if w == 0 else v_rows)[st.s]
                            mm = pe.matmul(to[w * WIN:(w + 1) * WIN, n * VW:(n + 1) * VW],
                                           probs_t[:, st.j % 2, n * P + w * WIN:n * P + (w + 1) * WIN],
                                           values[:, j, 4 * g + n, :], start=True, stop=True)
                    mm.then_inc(pe_o.of(st), 1)

                def turn_out(i, st, banks):
                    to = take(i, banks, 0)
                    pe.wait_ge(*dve_on.at(i, Step("o", st.s, st.l, 2 * st.j + 1, st.n)))
                    for c in range(PAIRS):
                        mm = pe.transpose(to[:, c * P:(c + 1) * P], o_rows[:, c * P:(c + 1) * P], ident)
                    mm.then_inc(pe_ot.of(st), 1)

                def project(i, st, banks):
                    to = take(i, banks, 0)
                    pe.wait_ge(*act_ot.at(i, Step("ot", st.s, st.l, st.j, st.n)))
                    for c in range(PAIRS):
                        mm = pe.matmul(to[:, 0:D], o_cols[:, c * P:(c + 1) * P], wo_sb[:, st.l, c, :],
                                       start=(c == 0), stop=(c == PAIRS - 1))
                    mm.then_inc(pe_wo.of(st), 1)

                def shift(i, st, banks):
                    to = take(i, banks, 0)
                    pe.wait_ge(*dve_wo.at(i, Step("wo", st.s, st.l, NT - 1, st.n)))
                    pe.matmul(to[:, 0:NT * DH], cst("shift"), x_res[st.s][:, :, DH:D], start=True, stop=True)
                    pe.matmul(to[:, DH:NT * DH], cst("wrap"), x_res[st.s][:, 0:NT - 1, DH:D],
                              start=False, stop=True, skip_group_check=True).then_inc(pe_sh.of(st), 1)

                def h2t(i, st, banks):
                    to = take(i, banks, 0)
                    pe.wait_ge(*dve_ln.at(i, Step("ln_ffn", st.s, st.l, 0, st.n)))
                    for j in range(NT):
                        mm = pe.transpose(to[:, j * P:(j + 1) * P], h2_rows[:, j, :], ident)
                    mm.then_inc(pe_h2t.of(st), 1)

                def up(i, st, banks):
                    pe.wait_ge(*act_h2t.at(i, Step("h2t", st.s, st.l, 0, st.n)))
                    for half in (1, 0):
                        for c, (at_, n) in enumerate(HID_CHUNKS):
                            to = take(i, banks, c + 3 * (1 - half))
                            pe.matmul(to[0:n, :], w1_sb[:, st.l, half * HID + at_:half * HID + at_ + n],
                                      h2_cols[:, :], start=True, stop=True).then_inc(pe_w1.of(st), 1)

                def down(i, st, banks):
                    to = take(i, banks, 0)
                    for c in range(3):
                        pe.wait_ge(*dve_u.at(i, Step("w1", st.s, st.l, 0, st.n), c + 1))
                    for j in range(NT):
                        for c, (_, n) in enumerate(HID_CHUNKS):
                            mm = pe.matmul(to[:, j * D:(j + 1) * D], hidden[0:n, c, j * P:(j + 1) * P],
                                           w2_sb[0:n, st.l, c, :], start=(c == 0), stop=(c == 2))
                    mm.then_inc(pe_w2.of(st), 1)

                does = {"yt": yt, "aqkv": aqkv, "at": at, "as": scores_linear, "ao": out_linear, "awo": awo, "h": h,
                        "qkv": qkv, "qkt": qkt, "s": scores, "pt": turn_probs, "o": mix, "ot": turn_out,
                        "wo": project, "sh": shift, "h2t": h2t, "w1": up, "w2": down}

                def run(i, steps, planned):
                    for st, banks in zip(steps, planned):
                        if st.kind in does:
                            does[st.kind](i, st, banks)

                whole_program(pe, run)

            @block.scalar
            def _(act):
                def copy(to, of):
                    return act.activation(to, of, ACT.Copy)

                def yt(i, st, b):
                    act.wait_ge(*pe_yt.at(i, st))
                    copy(y_cols[:, :], bank[b[0]][:, :]).then_inc(act_yt.of(st), 1)

                def aqkv(i, st, b):
                    act.wait_ge(*pe_aqkv.at(i, st))
                    copy(la_v[:, st.j, :], bank[b[0]][:, 2 * D:3 * D]).then_inc(act_av.of(st), 1)

                def slots_linear(i, st, b):
                    slots = la_vslot[:, st.j % 2, :, :].rearrange("p (g s) w -> p g (s w)", g=GROUPS)
                    values = la_v[:, st.j, :].rearrange("p (g s e) -> p g s e", g=GROUPS, s=SLOTS)
                    act.wait_ge(*act_av.at(i, Step("aqkv", st.s, 0, st.j, st.n)))
                    act.wait_ge(*pe_ao.at(i, Step("ao", st.s, 0, st.j, st.n), back=2))
                    for sl in range(SLOTS):
                        ins = copy(slots[:, :, sl * 32 + sl * LA_DH:sl * 32 + (sl + 1) * LA_DH],
                                   values[:, :, sl, :])
                    ins.then_inc(act_slots.of(st), 1)

                def exp_linear(i, st):
                    a = st.j % 2
                    act.wait_ge(*pool_ar.at(i, st))
                    act.wait_ge(*dve_aphi.at(i, st, back=2))
                    act.activation(la_ta[:, a, :], la_r[:, a, :], ACT.Exp).then_inc(act_aexp.of(st), 1)

                def at(i, st, b):
                    act.wait_ge(*pe_at.at(i, st))
                    act.wait_ge(*pe_ao.at(i, Step("ao", st.s, 0, st.j, st.n), back=2))
                    copy(la_qk_cols[:, st.j % 2, :], bank[b[0]][:, 0:2 * P]).then_inc(act_at.of(st), 1)

                def h(i, st, b):
                    act.wait_ge(*pe_h.at(i, st))
                    copy(h_cols[0:DH, :], bank[b[0]][0:DH, :]).then_inc(act_h.of(st), 1)
                    copy(h_cols[DH:P, 1:T], bank[b[0]][DH:P, 0:T - 1]).then_inc(act_h.of(st), 1)

                def qkv(i, st, b):
                    a = st.j % 2
                    act.wait_ge(*dve_rope.at(i, st, 5, back=1))
                    for w in range(2):
                        act.wait_ge(*pe_qkv.at(i, st, w + 1))
                        act.activation(qk_sq[:, w * INNER:(w + 1) * INNER], bank[b[w]][:, :],
                                       ACT.Square).then_inc(act_qkv.of(st), 1)
                    act.wait_ge(*pe_qkv.at(i, st, 3))
                    copy(v_rows[st.s][:, st.j, :, 0:DH], bank[b[2]][:, :].rearrange(
                        "p (h d) -> p h d", h=HEADS)).then_inc(act_qkv.of(st), 1)

                def qkt(i, st, b):
                    act.wait_ge(*pe_qkt.at(i, st, 1))
                    copy(q_cols[st.s][:, :, st.j * P:(st.j + 1) * P],
                         bank[b[0]][:, :].rearrange("p (c n) -> p c n", c=PAIRS)).then_inc(act_q.of(st), 1)

                def exps(i, st, b):
                    j, g, a = st.j // 2, st.j % 2, st.j % 2
                    act.wait_ge(*dve_max.at(i, st))
                    act.wait_ge(*pe_pt.at(i, st, back=2))
                    for n in range(4):
                        act.activation(probs[:, a, n * P:(n + 1) * P], bank[b[0]][:, n * P:(n + 1) * P], ACT.Exp,
                                       bias=s_bias[:, a, n:n + 1],
                                       scale=qk_rnorm[st.s][:, j, 4 * g + n:4 * g + n + 1]).then_inc(act_p.of(st), 1)

                def probs_turned(i, st, b):
                    act.wait_ge(*pe_pt.at(i, st))
                    act.wait_ge(*pe_o.at(i, st, back=2))
                    copy(probs_t[:, st.j % 2, :], bank[b[0]][:, :]).then_inc(act_pt.of(st), 1)

                def out_turned(i, st, b):
                    act.wait_ge(*pe_ot.at(i, st))
                    act.wait_ge(*pe_wo.at(i, st, back=1))
                    copy(o_cols[:, :], bank[b[0]][:, :]).then_inc(act_ot.of(st), 1)

                def shifted(i, st, b):
                    act.wait_ge(*dve_wo.at(i, Step("wo", st.s, st.l, NT - 1, st.n)))
                    copy(h2_rows[:, :, 0:DH], x_res[st.s][:, :, 0:DH]).then_inc(act_h2x.of(st), 1)

                def h2t(i, st, b):
                    act.wait_ge(*pe_h2t.at(i, st))
                    act.activation(h2_cols[:, :], bank[b[0]][:, :], ACT.Identity, bias=ln_cols[:, st.l, 1:2],
                                   scale=ln_cols[:, st.l, 0:1]).then_inc(act_h2t.of(st), 1)

                def gelus(i, st, b):
                    for c, (_, n) in enumerate(HID_CHUNKS):
                        act.wait_ge(*pe_w1.at(i, st, c + 1))
                        act.activation(hidden[0:n, c, :], bank[b[c]][0:n, :], ACT.Gelu,
                                       bias=b1_cols[0:n, st.l, 1, c:c + 1]).then_inc(act_gelu.of(st), 1)

                does = {"yt": yt, "aqkv": aqkv, "at": at, "as": slots_linear, "h": h, "qkv": qkv, "qkt": qkt, "s": exps,
                        "pt": probs_turned, "ot": out_turned, "sh": shifted, "h2t": h2t, "w1": gelus}

                def run(i, steps, planned):
                    for st, banks in zip(steps, planned):
                        if st.kind in does:
                            does[st.kind](i, st, [b for b, _ in banks])
                        if st.kind == "aqkv":
                            exp_linear(i, st)

                whole_program(act, run)

            @block.vector
            def _(dve):
                def stats(i, st, of):
                    s, o = st.s, order_of(st)
                    for j in range(NT):
                        dve.bn_stats(ln_stats[s][:, o, j, :], of(j)).then_inc(dve_ln.of(st), 1)
                    dve.wait_ge(*dve_ln.at(i, st, 4))
                    dve.memset(ln_held[s][:, o:o + 1], 0.0)
                    for j in range(NT):
                        dve.bn_aggr(ln_mv[s][:, o, j, :], ln_stats[s][:, o, j, :]).then_inc(dve_ln.of(st), 1)
                    dve.wait_ge(*dve_ln.at(i, st, 8))
                    dve.tensor_scalar(ln_var[s][:, o, :], ln_mv[s][:, o, :, 1], LN_EPS, None,
                                      ALU.add).then_inc(dve_ln.of(st), 1)

                def normed(i, st, of, to):
                    s, o = st.s, order_of(st)
                    dve.wait_ge(*pool_rstd.at(i, st))
                    for j in range(NT):
                        dve.tensor_scalar(to(j), of(j), ln_mv[s][:, o, j, 0:1], ln_rstd[s][:, o, j:j + 1],
                                          ALU.subtract, ALU.mult).then_inc(dve_ln.of(st), 1)

                def ln_in(i, st, b):
                    of = lambda j: x_io[st.s][:, j, :]
                    dve.wait_ge(*x_loaded.at(i, st, order=0))
                    stats(i, st, of)
                    normed(i, st, of, lambda j: y_rows[:, j, :])

                def ln_attn(i, st, b):
                    of = lambda j: bank[b[0]][:, j * D:(j + 1) * D]
                    dve.wait_ge(*pe_awo.at(i, Step("awo", st.s, n=st.n)))
                    stats(i, st, of)
                    normed(i, st, of, lambda j: y_rows[:, j, :])
                    dve.wait_ge(*dve_ln.at(i, st))
                    dve.tensor_tensor(x_io[st.s][:, :, :], x_io[st.s][:, :, :], y_rows[:, :, :],
                                      ALU.add).then_inc(dve_xmid.of(st), 1)

                def ln_mid(i, st, b):
                    of = lambda j: x_io[st.s][:, j, :]
                    dve.wait_ge(*dve_xmid.at(i, st, order=0))
                    stats(i, st, of)
                    normed(i, st, of, lambda j: x_res[st.s][:, j, :])

                def ln_ffn(i, st, b):
                    of = lambda j: h2_rows[:, j, :]
                    sh = Step("sh", st.s, st.l, 0, st.n)
                    dve.wait_ge(*dve_h2.at(i, sh))
                    dve.wait_ge(*act_h2x.at(i, sh))
                    stats(i, st, of)
                    normed(i, st, of, of)

                def ln_out(i, st, b):
                    of = lambda j: x_res[st.s][:, j, :]
                    dve.wait_ge(*dve_w2.at(i, Step("w2", st.s, DEPTH - 1, 0, st.n)))
                    stats(i, st, of)
                    normed(i, st, of, of)
                    dve.wait_ge(*dve_ln.at(i, st))
                    dve.tensor_tensor(x_io[st.s][:, :, :], x_res[st.s][:, :, :], x_io[st.s][:, :, :],
                                      ALU.add).then_inc(dve_out.of(st), 1)

                def rope_linear(i, st, b):
                    a, j = st.j % 2, st.j
                    qk = bank[b[0]][:, 0:2 * D]
                    cos = cst("la_cos")[:, j * LA_DH:(j + 1) * LA_DH]
                    sin = cst("la_sin")[:, j * LA_DH:(j + 1) * LA_DH].rearrange("p (t c) -> p t c", t=2)
                    dve.wait_ge(*act_av.at(i, st))
                    dve.wait_ge(*pool_ar.at(i, st, 1, back=2))
                    dve.wait_ge(*dve_aphi.at(i, st, back=2))
                    dve.tensor_tensor(la_ta[:, a, :].rearrange("p (h c) -> p h c", c=LA_DH),
                                      qk.rearrange("p (h c) -> p h c", c=LA_DH),
                                      cos.unsqueeze(1).to_broadcast([P, 2 * LA_HEADS, LA_DH]),
                                      ALU.mult).then_inc(dve_arope.of(st), 1)
                    dve.tensor_tensor(
                        la_tb[:, a, :].rearrange("p (h t c) -> p h t c", t=2, c=LA_DH // 2),
                        qk.rearrange("p (h t c) -> p h t c", t=2, c=LA_DH // 2)[:, :, ::-1, :],
                        sin.unsqueeze(1).to_broadcast([P, 2 * LA_HEADS, 2, LA_DH // 2]),
                        ALU.mult).then_inc(dve_arope.of(st), 1)

                def phi_linear(i, st):
                    a = st.j % 2
                    dve.wait_ge(*pool_ar.at(i, st))
                    dve.tensor_scalar(la_tb[:, a, :], la_r[:, a, :], 0.0, None, ALU.max).then_inc(dve_aphi.of(st), 1)
                    dve.wait_ge(*act_aexp.at(i, st))
                    dve.wait_ge(*dve_aphi.at(i, st, 1))
                    dve.scalar_tensor_tensor(out=la_phi[:, st.j, :], in0=la_ta[:, a, :], scalar=1.0,
                                             in1=la_tb[:, a, :], op0=ALU.min, op1=ALU.add).then_inc(dve_aphi.of(st), 1)

                def expand(i, st, b):
                    a = st.j % 2
                    dve.wait_ge(*act_at.at(i, st))
                    dve.wait_ge(*pe_as.at(i, Step("as", st.s, 0, st.j, st.n), back=2))
                    dve.tensor_tensor(la_qexp[:, a, :, :],
                                      la_qk_cols[:, a, 0:P].unsqueeze(1).to_broadcast([P, SLOTS, P]),
                                      cst("slot").unsqueeze(2).to_broadcast([P, SLOTS, P]),
                                      ALU.mult).then_inc(dve_qexp.of(st), 1)

                def mask_linear(i, st, b):
                    a = st.j % 2
                    dve.wait_ge(*pe_ao.at(i, Step("ao", st.s, 0, st.j, st.n), back=2))
                    for g in range(GROUPS):
                        dve.wait_ge(*pe_as.at(i, st, g + 1))
                        dve.tensor_tensor(la_sm[:, a, g, :, :],
                                          bank[b[g]][:, :].rearrange("p (s q) -> p s q", s=SLOTS),
                                          cst("causal").unsqueeze(1).to_broadcast([P, SLOTS, P]),
                                          ALU.mult).then_inc(dve_sm.of(st), 1)

                def out_linear(i, st, b):
                    s, j, of = st.s, st.j, bank[b[0]]
                    dve.wait_ge(*pe_ao.at(i, st))
                    if j < NT - 1:
                        dve.wait_ge(*dve_state.at(i, st, back=1, order=j))
                        dve.tensor_tensor(la_tmp[:, :], of[:, 256:512], cst("block"),
                                          ALU.mult).then_inc(dve_state.of(st), 1)
                        dve.wait_ge(*dve_state.at(i, st, 1, order=j))
                        dve.tensor_tensor(la_state[s][:, :], la_tmp[:, :],
                                          cst("zeros").to_broadcast([P, 2 * D]) if j == 0 else la_state[s][:, :],
                                          ALU.add).then_inc(dve_state.of(st), 1)
                    dve.wait_ge(*dve_ao.at(i, st, back=1))
                    dve.tensor_scalar(la_den[:, :], of[:, P:2 * P], DEN_EPS, None, ALU.max).then_inc(dve_ao.of(st), 1)
                    dve.wait_ge(*dve_ao.at(i, st, 1))
                    dve.reciprocal(la_den[:, :], la_den[:, :]).then_inc(dve_ao.of(st), 1)
                    dve.wait_ge(*dve_ao.at(i, st, 2))
                    dve.tensor_tensor(y_cols[:, j * P:(j + 1) * P], of[:, 0:P], la_den[:, :],
                                      ALU.mult).then_inc(dve_ao.of(st), 1)

                def rope_softmax(i, st, b):
                    s, l, j, a = st.s, st.l, st.j, st.j % 2
                    dve.wait_ge(*pe_qkt.at(i, Step("qkt", s, l, j, st.n), back=2))
                    for w in range(2):
                        dve.wait_ge(*act_qkv.at(i, st, w + 1))
                        of = bank[b[w]][:, :]
                        cos = rope[:, l, 2 * w, j * DH:(j + 1) * DH]
                        sin = rope[:, l, 2 * w + 1, j * DH:(j + 1) * DH].rearrange("p (t c) -> p t c", t=2)
                        dve.tensor_tensor(qk_t[:, a, w, 0, :].rearrange("p (h c) -> p h c", c=DH),
                                          of.rearrange("p (h c) -> p h c", c=DH),
                                          cos.unsqueeze(1).to_broadcast([P, HEADS, DH]),
                                          ALU.mult).then_inc(dve_rope.of(st), 1)
                        dve.tensor_tensor(
                            qk_t[:, a, w, 1, :].rearrange("p (h t c) -> p h t c", t=2, c=DH // 2),
                            of.rearrange("p (h t c) -> p h t c", t=2, c=DH // 2)[:, :, ::-1, :],
                            sin.unsqueeze(1).to_broadcast([P, HEADS, 2, DH // 2]),
                            ALU.mult).then_inc(dve_rope.of(st), 1)
                    dve.tensor_reduce(qk_ss[s][:, j, :], qk_sq.rearrange("p (h c) -> p h c", c=DH), AX.X,
                                      ALU.add).then_inc(dve_rope.of(st), 1)
                    dve.wait_ge(*dve_rope.at(i, st, 5))
                    dve.tensor_scalar(qk_ss[s][:, j, :], qk_ss[s][:, j, :], NORM_EPS ** 2, None,
                                      ALU.max).then_inc(dve_rope.of(st), 1)

                def keys_turned(i, st, b):
                    j = st.j
                    dve.wait_ge(*pe_qkt.at(i, st, 2))
                    for half in range(2):
                        rows = slice(half * DH, (half + 1) * DH)
                        dve.tensor_copy(k_windows(k_cols[st.s][rows, :, half, :], WIN, j * WIN),
                                        bank[b[1]][rows, :].rearrange("p (c e n) -> p c e n", c=PAIRS, e=2)
                                        ).then_inc(dve_k.of(st), 1)

                def maxima(i, st, b):
                    j, g, a = st.j // 2, st.j % 2, st.j % 2
                    dve.wait_ge(*pe_s.at(i, st))
                    dve.wait_ge(*act_p.at(i, st, back=2))
                    dve.tensor_reduce(s_max[:, a, :], bank[b[0]][:, :].rearrange("p (h k) -> p h k", h=4), AX.X,
                                      ALU.max).then_inc(dve_max.of(st), 1)
                    if g == 0:
                        dve.wait_ge(*pool_rnorm.at(i, Step("qkv", st.s, st.l, j, st.n)))
                    dve.wait_ge(*dve_max.at(i, st, 1))
                    dve.scalar_tensor_tensor(out=s_bias[:, a, :], in0=s_max[:, a, :], scalar=-1.0,
                                             in1=qk_rnorm[st.s][:, j, 4 * g:4 * g + 4], op0=ALU.mult,
                                             op1=ALU.mult).then_inc(dve_max.of(st), 1)

                def divide(i, st, b):
                    j, g, a = st.j // 2, st.j % 2, st.j % 2
                    of = bank[b[0]][:, 0:4 * VW].rearrange("p (h c) -> p h c", c=VW)
                    dve.wait_ge(*pe_o.at(i, st))
                    dve.wait_ge(*dve_on.at(i, st, back=2))
                    dve.reciprocal(o_rden[:, a, :], of[:, :, DH]).then_inc(dve_on.of(st), 1)
                    if g == 0:
                        dve.wait_ge(*pe_ot.at(i, Step("ot", st.s, st.l, j, st.n), back=1))
                    dve.wait_ge(*dve_on.at(i, st, 1))
                    dve.tensor_tensor(
                        o_rows[:, g * 256:(g + 1) * 256].rearrange("p (h c) -> p h c", c=DH), of[:, :, 0:DH],
                        o_rden[:, a, :].unsqueeze(2).to_broadcast([P, 4, DH]), ALU.mult).then_inc(dve_on.of(st), 1)

                def add_attention(i, st, b):
                    x_tile = x_res[st.s][:, st.j, :]
                    dve.wait_ge(*pe_wo.at(i, st))
                    dve.tensor_tensor(x_tile, x_tile, bank[b[0]][:, 0:D], ALU.add).then_inc(dve_wo.of(st), 1)

                def shifted(i, st, b):
                    dve.wait_ge(*pe_sh.at(i, st))
                    dve.tensor_copy(h2_rows[:, :, DH:D], bank[b[0]][:, 0:NT * DH].rearrange(
                        "p (j c) -> p j c", j=NT)).then_inc(dve_h2.of(st), 1)

                def gate(i, st, b):
                    for c, (_, n) in enumerate(HID_CHUNKS):
                        dve.wait_ge(*pe_w1.at(i, st, 4 + c))
                        dve.wait_ge(*act_gelu.at(i, st, c + 1))
                        dve.scalar_tensor_tensor(out=hidden[0:n, c, :], in0=bank[b[3 + c]][0:n, :],
                                                 scalar=b1_cols[0:n, st.l, 0, c:c + 1], in1=hidden[0:n, c, :],
                                                 op0=ALU.add, op1=ALU.mult).then_inc(dve_u.of(st), 1)

                def add_ffn(i, st, b):
                    x_all = x_res[st.s][:, :, :]
                    dve.wait_ge(*pe_w2.at(i, st))
                    dve.wait_ge(*pool_b2.at(i, Step("sh", st.s, st.l, 0, st.n)))
                    dve.tensor_tensor(x_all, x_all, bank[b[0]][:, :].rearrange("p (j c) -> p j c", j=NT),
                                      ALU.add).then_inc(dve_w2.of(st), 1)

                does = {"ln_in": ln_in, "ln_attn": ln_attn, "ln_mid": ln_mid, "ln_ffn": ln_ffn, "ln_out": ln_out,
                        "aqkv": rope_linear, "at": expand, "as": mask_linear, "ao": out_linear, "qkv": rope_softmax,
                        "qkt": keys_turned, "s": maxima, "o": divide, "wo": add_attention, "sh": shifted,
                        "w1": gate, "w2": add_ffn}

                def run(i, steps, planned):
                    projected = {}
                    for st, banks in zip(steps, planned):
                        b = [x for x, _ in banks]
                        if st.kind == "awo":
                            projected[st.s] = b
                        if st.kind == "ln_attn":
                            b = projected[st.s]
                        if st.kind in does:
                            does[st.kind](i, st, b)
                        if st.kind == "aqkv":
                            phi_linear(i, st)

                whole_program(dve, run)

            @block.gpsimd
            def _(pool):
                def rstd(i, st):
                    s, o = st.s, order_of(st)
                    pool.wait_ge(*dve_ln.at(i, st, 9))
                    pool.tensor_tensor(ln_rstd[s][:, o, :], ln_var[s][:, o, :], minus_half[:, 0:NT],
                                       ALU.pow).then_inc(pool_rstd.of(st), 1)

                def rotate_linear(i, st):
                    a = st.j % 2
                    pool.wait_ge(*dve_arope.at(i, st))
                    pool.wait_ge(*dve_aphi.at(i, st, back=2))
                    pool.tensor_tensor(la_r[:, a, :], la_ta[:, a, :], la_tb[:, a, :],
                                       ALU.add).then_inc(pool_ar.of(st), 1)

                def rotate_softmax(i, st):
                    s, j, a = st.s, st.j, st.j % 2
                    heads = lambda t: t.rearrange("p (h c) -> p h c", c=DH)
                    pool.wait_ge(*dve_rope.at(i, st, 2))
                    pool.tensor_tensor(qk_t[:, a, 0, 0, :], qk_t[:, a, 0, 0, :], qk_t[:, a, 0, 1, :],
                                       ALU.add).then_inc(pool_qk.of(st), 1)
                    pool.wait_ge(*dve_rope.at(i, st, 4))
                    pool.tensor_tensor(qk_t[:, a, 1, 0, :], qk_t[:, a, 1, 0, :], qk_t[:, a, 1, 1, :],
                                       ALU.add).then_inc(pool_qk.of(st), 1)
                    pool.wait_ge(*dve_rope.at(i, st, 6))
                    pool.tensor_tensor(qk_rnorm[s][:, j, :], qk_ss[s][:, j, :], minus_half[:, :],
                                       ALU.pow).then_inc(pool_rnorm.of(st), 1)
                    pool.wait_ge(*pool_rnorm.at(i, st))
                    pool.wait_ge(*pool_qk.at(i, st, 2))
                    pool.tensor_tensor(heads(qk_t[:, a, 1, 0, :]), heads(qk_t[:, a, 1, 0, :]),
                                       qk_rnorm[s][:, j, HEADS:2 * HEADS].unsqueeze(2).to_broadcast([P, HEADS, DH]),
                                       ALU.mult).then_inc(pool_qk.of(st), 1)
                    pool.wait_ge(*act_qkv.at(i, st, 3))
                    pool.wait_ge(*pool_qk.at(i, st, 3))
                    ones = cst("ones").to_broadcast([P, HEADS * VW]).rearrange("p (h c) -> p h c", c=VW)
                    low, high = v_rows[s][0:WIN, j, :, :], v_rows[s][WIN:P, j, :, :]
                    pool.tensor_tensor(v_even[s][0:WIN, j, :, :], low, ones[0:WIN], ALU.mult).then_inc(pool_ve.of(st), 1)
                    pool.wait_ge(*pool_ve.at(i, st, 1))
                    if j < NT - 1:
                        pool.tensor_tensor(v_even[s][WIN:P, j + 1, :, :], high, ones[WIN:P],
                                           ALU.mult).then_inc(pool_ve.of(st), 1)
                    else:
                        pool.sem_inc(pool_ve.of(st), 1)
                    pool.wait_ge(*pool_ve.at(i, st))

                def bias(i, st):
                    x_all = x_res[st.s][:, :, :]
                    pool.wait_ge(*pe_sh.at(i, st))
                    pool.wait_ge(*act_h2x.at(i, st))
                    pool.tensor_tensor(x_all, x_all, b2_rows[:, st.l, :].unsqueeze(1).to_broadcast([P, NT, D]),
                                       ALU.add).then_inc(pool_b2.of(st), 1)

                does = {"aqkv": rotate_linear, "qkv": rotate_softmax, "sh": bias}
                does.update({k: rstd for k in LN_ORDER})

                def run(i, steps, planned):
                    for st in steps:
                        if st.kind in does:
                            does[st.kind](i, st)

                whole_program(pool, run)


_INS = ["L0_attn_x", "L0_attn_Wq", "L0_attn_Wk", "L0_attn_Wv", "L0_attn_Wo", "L0_ffn_wqkv", "L0_ffn_q_scale",
        "L0_ffn_k_scale", "L0_ffn_wo", "L0_ffn_ln_g", "L0_ffn_ln_b", "L0_ffn_w1", "L0_ffn_b1", "L0_ffn_w2", "L0_ffn_b2"]


def kernel(**inputs):
    import concourse.bacc as bacc
    from concourse.bass_utils import run_bass_kernel_spmd

    nc = bacc.Bacc("TRN2", target_bir_lowering=False, num_devices=1)
    arrays = {f"in_{name}": np.ascontiguousarray(inputs[name]) for name in _INS}
    arrays["in_constants"] = CONSTANTS
    args = [nc.dram_tensor(n, a.shape, mybir.dt.from_np(a.dtype), kind="ExternalInput").ap() for n, a in arrays.items()]
    args.append(nc.dram_tensor("out_0", (B, T, D), mybir.dt.float32, kind="ExternalOutput").ap())
    build(nc, *args)
    r = run_bass_kernel_spmd(nc, [arrays], core_ids=[0])
    return r.results[0]["out_0"]
```

```python
from contextlib import ExitStack

import numpy as np

import concourse.bass as bass
from concourse import mybir

B, T, D = 16, 512, 128
P = 128
NT = T // P
STREAMS = 2
ROUNDS = B // STREAMS
LA_HEADS, LA_DH = 16, 8
GROUPS, SLOTS = 4, 4
DEPTH, HEADS, DH, WIN = 2, 8, 64, 64
INNER = HEADS * DH
PAIRS = HEADS // 2
HID = int(D * 4 * 2 / 3)
HID_CHUNKS = [(0, 128), (128, 128), (256, HID - 256)]
UNITS = NT * 2
QK_SCALE = 8.0
KPAD = 576
ODD = 256
VW = DH + 1
MASKED = -float(2.0 ** 100)
LN_EPS, DEN_EPS, NORM_EPS = 1e-5, 1e-6, 1e-12
BANKS = 8
W_SCALE = 64.0
PASSES = [(0, 0), (0, 1), (1, 0)]

CONST_COLS = {}
SETUP_ONLY = ("mask_first", "mask_later", "q_cos", "q_sin", "k_cos", "k_sin")


def _constants():
    f = np.float32
    p = np.arange(P)
    parts = []

    def put(name, a):
        a = np.ascontiguousarray(np.asarray(a, f).reshape(P, -1))
        CONST_COLS[name] = (sum(x.shape[1] for x in parts), a.shape[1])
        parts.append(a)

    put("ident", np.eye(P))
    put("shift", np.eye(P, k=1))
    wrap = np.zeros((P, P), f)
    wrap[P - 1, 0] = 1
    put("wrap", wrap)
    put("causal", (p[:, None] <= p[None, :]))
    put("block", np.tile(p[:, None] // LA_DH == p[None, :] // LA_DH, (1, 2)))
    put("slot", (p[:, None] // LA_DH) % SLOTS == np.arange(SLOTS)[None, :])
    put("ones_slot", np.tile((np.arange(SLOTS)[:, None] == (np.arange(32) // LA_DH)[None, :])[None], (P, 1, 1)))
    put("ones", np.ones((P, 1)))
    put("zeros", np.zeros((P, 1)))
    half = LA_DH // 2
    inv = (f(10000.0) ** (-np.arange(half, dtype=f) / f(half))).astype(f)
    ang = (np.arange(T, dtype=f)[:, None] * inv[None, :]).astype(f)
    c, s = np.cos(ang), np.sin(ang)
    rows = lambda a: a.reshape(NT, P, -1).transpose(1, 0, 2)
    put("la_cos", rows(np.concatenate([c, c], 1)))
    put("la_sin", rows(np.concatenate([-s, s], 1)))
    q, k = np.arange(WIN)[:, None], np.arange(WIN)[None, :]
    own, before = np.where(k <= q, 0, MASKED), np.where(k >= q, 0, MASKED)
    later = np.concatenate([np.concatenate([own, before], 1), np.concatenate([before, own], 1)], 0)
    first = later.copy()
    first[:WIN, WIN:] = MASKED
    put("mask_first", np.tile(first, (1, 4)))
    put("mask_later", np.tile(later, (1, 4)))
    idx = np.arange(0, DH, 2, dtype=f)
    inv = (f(1.0) / f(10000.0) ** (idx / f(DH))).astype(f)
    t = np.arange(T, dtype=f)
    ang = (t[:, None] * inv[None, :]).astype(f)
    base = ((idx + f(0.4 * DH)) / f(1.4 * DH)).astype(f)
    scale = (base[None, :] ** ((t - T // 2) / f(WIN // 2))[:, None]).astype(f)
    c, s = np.cos(ang), np.sin(ang)
    put("q_cos", rows(np.concatenate([c * scale, c * scale], 1)))
    put("q_sin", rows(np.concatenate([-s * scale, s * scale], 1)))
    put("k_cos", rows(np.concatenate([c / scale, c / scale], 1)))
    put("k_sin", rows(np.concatenate([-s / scale, s / scale], 1)))
    return np.concatenate(parts, 1)


CONSTANTS = _constants()
NCONST = CONST_COLS["mask_first"][0]
NSETUP = CONSTANTS.shape[1] - NCONST


class Step:

    def __init__(self, kind, s, l=0, j=0, n=0):
        self.kind, self.s, self.l, self.j, self.n = kind, s, l, j, n

    def moved(self, by):
        return Step(self.kind, self.s, self.l, self.j, self.n + by)


SPAN = {"qkv_tile": 4.2, "yt": 0.53, "awo": 1.5, "h": 1.5, "sh": 4, "h2t": 1.5, "w1": 7.2, "w2": 3.5, "ln_in": 1.18,
        "norm_in": 2, "ln_attn": 1.5, "norm_attn": 1.5, "ln_mid": 2.55, "norm_mid": 1.4, "ln_ffn": 3,
        "norm_ffn": 1.4, "ln_out": 4.2, "norm_out": 1.4}
LAG = {"phi": 0.85, "at": 1.67, "as": 2.79, "ao": 3.3, "qkt": 1.7, "pt": 1.56, "o": 2.34, "ot": 3.09, "wo": 4.27}
ROUND = 282
PHASES = [{"before": (9.0, 16.9), "linear": (20.7, 54.4), "after": (27.2, 62.6), "qkv0": (62.7, 89.9),
           "attn0": (87.2, 142.4), "ffn0": (142.4, 187.9), "qkv1": (182.8, 229.0), "attn1": (224.7, 262.0),
           "ffn1": (266.2, 281.3)},
          {"before": (93.5, 98.8), "linear": (98.8, 148.9), "after": (145.4, 146.3), "qkv0": (148, 176.9),
           "attn0": (176.8, 214.1), "ffn0": (214.1, 229), "qkv1": (229, 281.8), "attn1": (269.5, 327.7),
           "ffn1": (335.9, 363.9)}]


BEHIND = {"tensor": {},
          "vector": {"qkv": 2.5, "s": 1.5, "o": 0.5, "w1": 2.72, "aqkv": 1.35, "qkt": 0.5, "wo": 0.5},
          "scalar": {"qkv": 1, "s": 2.5, "pt": 0.77, "ot": 0.3, "qkt": 0.5, "w1": 1, "aqkv": 0.68, "as": 0.4},
          "gpsimd": {"qkv": 3, "aqkv": 1.27, "ln_attn": 0.7, "sh": 0.74}}
HOLD = {"yt": 1.8, "aqkv": 6, "at": 1.8, "as": 3.5, "ao": 4, "awo": 5.04, "h": 2, "qkv": 6, "qkt": 2.04, "s": 6.0,
        "pt": 1.5, "o": 2, "ot": 1.8, "wo": 1.5, "sh": 2.4, "h2t": 2, "w1": 8, "w2": 3}


def one_by_one(s, l, kinds):
    out, at = [], 0.0
    for kind in kinds:
        out.append((at, Step(kind, s, l)))
        at += SPAN[kind]
    return out, at


def pipelined(s, l, kinds, count):
    out = [(j + LAG.get(kind, 0), Step(kind, s, l, j)) for kind in kinds for j in range(count)]
    return out, count + LAG.get(kinds[-1], 0)


def phase(s, name):
    if name == "before":
        return one_by_one(s, 0, ("ln_in", "norm_in", "yt"))
    if name == "linear":
        return pipelined(s, 0, ("aqkv", "phi", "at", "as", "ao"), NT)
    if name == "after":
        return one_by_one(s, 0, ("awo", "ln_attn", "norm_attn", "ln_mid", "norm_mid"))
    l = int(name[-1])
    if name.startswith("qkv"):
        before, t0 = one_by_one(s, l, ("h",))
        tiles, t1 = pipelined(s, l, ("qkv", "qkt"), NT)
        per_tile = SPAN["qkv_tile"]
        return before + [(t0 + t * per_tile, x) for t, x in tiles], t0 + (t1 + 0.5) * per_tile
    if name.startswith("attn"):
        out, _ = pipelined(s, l, ("s", "pt", "o"), UNITS)
        for kind in ("ot", "wo"):
            out += [(2 * j + 1 + LAG[kind], Step(kind, s, l, j)) for j in range(NT)]
        return out, UNITS + LAG["wo"]
    kinds = ("sh", "ln_ffn", "norm_ffn", "h2t", "w1", "w2") + (("ln_out", "norm_out") if l == DEPTH - 1 else ())
    return one_by_one(s, l, kinds)


def window(engine):
    placed = []
    for s in range(STREAMS):
        at = latest = -1.0
        for name, (start, end) in PHASES[s].items():
            steps, whole = phase(s, name)
            if name.startswith("attn"):
                at = latest = -1.0
            for t, step in sorted(steps, key=lambda x: (x[0], -x[1].j)):
                at = max(at, start + t / whole * (end - start))
                mine = at + BEHIND[engine].get(step.kind, 0)
                if step.kind in SPAN:
                    mine = max(mine, latest)
                latest = max(latest, mine)
                placed.append((mine % ROUND, s, len(placed), step.moved(-int(mine // ROUND))))
    return [(x[0], x[3]) for x in sorted(placed, key=lambda x: x[:3])]


def name_of(step):
    return step.kind, step.s, step.l, step.j


def banks_of(steps, count):
    free, banks = [0.0] * BANKS, {}
    for turn in range(2):
        for time, step in steps:
            banks[name_of(step)] = []
            for _ in range(count.get(step.kind, 0)):
                b = min(range(BANKS), key=lambda b: (free[b], b))
                banks[name_of(step)].append(b)
                free[b] = time + HOLD[step.kind]
        free = [f - ROUND for f in free]
    return banks


LN_ORDER = {"ln_in": 0, "ln_attn": 1, "ln_mid": 2, "ln_ffn": 3, "ln_out": 5}
LN_ORDER.update({k.replace("ln_", "norm_"): n for k, n in LN_ORDER.items()})


def order_of(step):
    if step.kind in LN_ORDER:
        return LN_ORDER[step.kind] + (step.l if step.kind.endswith("_ffn") else 0)
    return step.l * tiles_of(step.kind) + step.j


def tiles_of(kind):
    if kind in ("s", "pt", "o"):
        return UNITS
    if kind in ("qkv", "qkt", "ot", "wo", "aqkv", "phi", "at", "as", "ao"):
        return NT
    return 1


def steps_of(kind):
    if kind in LN_ORDER:
        return 6
    return tiles_of(kind) * (DEPTH if kind in ("h", "qkv", "qkt", "s", "pt", "o", "ot", "wo", "sh", "h2t", "w1", "w2") else 1)


class Signal:

    def __init__(self, nc, ctx, name, kind, incs=1, per_inc=1, steps=None):
        self.steps = steps_of(kind) if steps is None else steps
        self.incs, self.per_inc = incs, per_inc
        self.sems = [ctx.enter_context(nc.semaphore(f"{name}_{s}")) for s in range(STREAMS)]

    def start(self):
        return self.steps * self.incs * self.per_inc

    def of(self, step):
        return self.sems[step.s]

    def at(self, i, step, k=None, back=0, order=None):
        k = self.incs if k is None else k
        order = order_of(step) if order is None else order
        fixed = (((step.n + 1) * self.steps + order - back) * self.incs + k) * self.per_inc
        return self.sems[step.s], i.times(self.start()) + fixed


class Round:

    def __init__(self, eng, i):
        self.eng, self.i, self.kept = eng, i, {}

    def times(self, by):
        if isinstance(self.i, int):
            return self.i * by
        if by not in self.kept:
            self.kept[by] = self.eng.snap(self.i * by)
        return self.kept[by]


def build(nc, x, wq, wk, wv, wo_la, wqkv, q_scale, k_scale, wo, ln_g, ln_b, w1, b1, w2, b2, consts, out):
    f32, bf16, f16 = mybir.dt.float32, mybir.dt.bfloat16, mybir.dt.float16
    ALU, ACT, AX = mybir.AluOpType, mybir.ActivationFunctionType, mybir.AxisListType
    ctx = ExitStack()
    nc.disable_value_cache = True

    with ctx:
        def sb(name, shape, dt=f32):
            return ctx.enter_context(nc.sbuf_tensor(name, shape, dt))

        const = sb("const", [P, NCONST])
        setup_const = None

        def cst(name):
            at, n = CONST_COLS[name]
            return setup_const[:, at - NCONST:at - NCONST + n] if name in SETUP_ONLY else const[:, at:at + n]

        ident = cst("ident")
        ident_h = sb("ident_h", [P, P], bf16)
        mask_h = sb("mask_h", [P, 2, 4 * P], bf16)
        w_la = sb("w_la", [P, 3 * D])
        wo_la_t = sb("wo_la_t", [P, D])
        wqkv_sb = sb("wqkv_sb", [P, DEPTH, 2, 3 * INNER], f16)
        wo_sb = sb("wo_sb", [P, DEPTH, PAIRS, D])
        w1_sb = sb("w1_sb", [P, DEPTH, 2, 2 * HID], f16)
        w2_sb = sb("w2_sb", [P, DEPTH, 3, D])
        b2_rows = sb("b2_rows", [P, DEPTH, D])
        b1_cols = sb("b1_cols", [P, DEPTH, 2, 3])
        ln_cols = sb("ln_cols", [P, DEPTH, 2])
        rope = sb("rope", [P, DEPTH, 4, NT * DH])
        minus_half = sb("minus_half", [P, 16])

        x_io = [sb(f"x_io{s}", [P, NT, D]) for s in range(STREAMS)]
        x_res = [sb(f"x_res{s}", [P, NT, D]) for s in range(STREAMS)]
        q_cols = [sb(f"q_cols{s}", [P, PAIRS, T]) for s in range(STREAMS)]
        k_cols = [sb(f"k_cols{s}", [P, PAIRS, 2, KPAD]) for s in range(STREAMS)]
        v_rows = [sb(f"v_rows{s}", [P, NT, HEADS, VW]) for s in range(STREAMS)]
        v_even = [sb(f"v_even{s}", [P, NT, HEADS, VW]) for s in range(STREAMS)]
        qk_rnorm = [sb(f"qk_rnorm{s}", [P, NT, 2 * HEADS]) for s in range(STREAMS)]
        qk_ss = [sb(f"qk_ss{s}", [P, NT, 2 * HEADS]) for s in range(STREAMS)]
        ln_stats = [sb(f"ln_stats{s}", [P, 6, NT, 6]) for s in range(STREAMS)]
        ln_mv = [sb(f"ln_mv{s}", [P, 6, NT, 2]) for s in range(STREAMS)]
        ln_var = [sb(f"ln_var{s}", [P, 6, NT]) for s in range(STREAMS)]
        ln_rstd = [sb(f"ln_rstd{s}", [P, 6, NT]) for s in range(STREAMS)]
        ln_held = [sb(f"ln_held{s}", [P, 6]) for s in range(STREAMS)]
        la_state = [sb(f"la_state{s}", [P, 2 * D]) for s in range(STREAMS)]

        y_rows = sb("y_rows", [P, NT, D])
        y_cols = sb("y_cols", [P, T])
        la_ta = sb("la_ta", [P, 2, 2 * D])
        la_tb = sb("la_tb", [P, 2, 2 * D])
        la_phi = sb("la_phi", [P, NT, 2 * D])
        la_v = sb("la_v", [P, NT, D])
        la_vslot = sb("la_vslot", [P, 2, LA_HEADS, 32])
        la_qk_cols = sb("la_qk_cols", [P, 2, 2 * P])
        la_den = sb("la_den", [P, P])
        la_tmp = sb("la_tmp", [P, 2 * D])
        room = sb("room", [P, 5120])
        la_qexp = room[:, 0:1024].rearrange("p (a s q) -> p a s q", a=2, s=SLOTS)
        la_sm = room[:, 1024:5120].rearrange("p (a g s q) -> p a g s q", a=2, g=GROUPS, s=SLOTS)
        qk_sq = room[:, 0:1024]
        qk_t = room[:, 1024:5120].rearrange("p (a w c n) -> p a w c n", a=2, w=2, c=2)
        h_cols = sb("h_cols", [P, 2, T], f16)
        probs = sb("probs", [P, 3, 4 * P])
        probs_t = sb("probs_t", [P, 2, 4 * P])
        s_max = [sb(f"s_max{s}", [P, UNITS, 4]) for s in range(STREAMS)]
        s_bias = [sb(f"s_bias{s}", [P, UNITS, 4]) for s in range(STREAMS)]
        o_rden = [sb(f"o_rden{s}", [P, UNITS, 4]) for s in range(STREAMS)]
        o_rows = sb("o_rows", [P, INNER])
        o_cols = sb("o_cols", [P, INNER])
        h2_rows = sb("h2_rows", [P, NT, D])
        h2_whole = h2_rows[:, :, :].rearrange("p j d -> p (j d)")
        h2_cols = sb("h2_cols", [P, 2, T], f16)
        hidden = sb("hidden", [P, 3, T])

        def k_windows(of, ahead, first):
            ap = of[..., first:first + WIN]
            return bass.AP(tensor=ap.tensor, offset=ap.offset, ap=[*ap.ap[:-1], [ODD + ahead, 2], list(ap.ap[-1])])

        def turned_keys(copy, st, b, half):
            rows = slice(half * DH, (half + 1) * DH)
            return copy(k_windows(k_cols[st.s][rows, :, half, :], WIN, st.j * WIN),
                        bank[b[0]][rows, :].rearrange("p (c e n) -> p c e n", c=PAIRS, e=2))

        bank = [ctx.enter_context(nc.psum_tensor(f"bank{b}", [P, 512], f32)) for b in range(BANKS)]

        def signal(name, kind, incs=1, per_inc=1, steps=None):
            return Signal(nc, ctx, name, kind, incs, per_inc, steps)

        pe_yt = signal("pe_yt", "yt")
        pe_aqkv = signal("pe_aqkv", "aqkv")
        pe_at = signal("pe_at", "at")
        pe_as = signal("pe_as", "as", GROUPS)
        pe_ao = signal("pe_ao", "ao")
        pe_awo = signal("pe_awo", "awo")
        pe_h = signal("pe_h", "h")
        pe_qkv = signal("pe_qkv", "qkv", 3)
        pe_qkt = signal("pe_qkt", "qkt", 2)
        pe_s = signal("pe_s", "s")
        pe_pt = signal("pe_pt", "pt")
        pe_o = signal("pe_o", "o")
        pe_ot = signal("pe_ot", "ot")
        pe_wo = signal("pe_wo", "wo")
        pe_sh = signal("pe_sh", "sh")
        pe_h2t = signal("pe_h2t", "h2t")
        pe_w1 = signal("pe_w1", "w1", 6)
        pe_w2 = signal("pe_w2", "w2")
        act_yt = signal("act_yt", "yt")
        act_av = signal("act_av", "aqkv")
        act_slots = signal("act_slots", "as")
        act_aexp = signal("act_aexp", "aqkv")
        act_at = signal("act_at", "at")
        act_h = signal("act_h", "h", 2)
        act_qkv = signal("act_qkv", "qkv", 5)
        act_k = signal("act_k", "qkt")
        act_q = signal("act_q", "qkt")
        act_p = signal("act_p", "s", 4)
        act_pt = signal("act_pt", "pt")
        act_ot = signal("act_ot", "ot")
        act_h2x = signal("act_h2x", "sh")
        act_h2t = signal("act_h2t", "h2t", 2)
        act_gelu = signal("act_gelu", "w1", 3)
        dve_ln = signal("dve_ln", "ln_in", 4 + 4 + 1 + 4)
        dve_arope = signal("dve_arope", "aqkv", 2)
        dve_aphi = signal("dve_aphi", "aqkv", 2)
        dve_sm = signal("dve_sm", "as", GROUPS)
        dve_ao = signal("dve_ao", "ao", 3)
        dve_state = signal("dve_state", "ao", 2, steps=NT - 1)
        dve_xmid = signal("dve_xmid", "ln_attn", steps=1)
        dve_rope = signal("dve_rope", "qkv", 4)
        dve_k_rotated = signal("dve_k_rotated", "qkv")
        dve_ss = signal("dve_ss", "qkv", 2)
        dve_k = signal("dve_k", "qkt")
        dve_max = signal("dve_max", "s", 2)
        dve_on = signal("dve_on", "o", 2)
        dve_h = signal("dve_h", "h", 2)
        dve_h2t = signal("dve_h2t", "h2t")
        dve_wo = signal("dve_wo", "wo")
        dve_h2 = signal("dve_h2", "sh")
        dve_u = signal("dve_u", "w1", 3)
        dve_w2 = signal("dve_w2", "w2")
        dve_out = signal("dve_out", "ln_out", steps=1)
        pool_rstd = signal("pool_rstd", "ln_in")
        pool_qexp = signal("pool_qexp", "at")
        pool_ar = signal("pool_ar", "aqkv")
        pool_rnorm = signal("pool_rnorm", "qkv", 2)
        pool_qk = signal("pool_qk", "qkv", 2)
        pool_b2 = signal("pool_b2", "sh")
        x_loaded = signal("x_loaded", "ln_in", 1, 16, steps=1)
        out_stored = signal("out_stored", "ln_out", 1, 16, steps=1)
        every = [v for v in list(locals().values()) if isinstance(v, Signal)]

        RELEASED = {
            "yt": [(act_yt, 1)], "aqkv": [(dve_arope, 2)], "at": [(act_at, 1)],
            "as": [(dve_sm, g + 1) for g in range(GROUPS)], "ao": [(dve_ao, 3)], "awo": [(dve_ln, 13)],
            "h": [(dve_h, 2)], "qkv": [(dve_rope, 4), (dve_rope, 2), (act_qkv, 5)],
            "qkt": [(dve_k, 1, act_k, 1), (act_q, 1)], "s": [(act_p, 4)], "pt": [(act_pt, 1)], "o": [(dve_on, 2)],
            "ot": [(act_ot, 1)], "wo": [(dve_wo, 1)], "sh": [(dve_h2, 1)], "h2t": [(act_h2t, 2)],
            "w1": [(act_gelu, c + 1) for c in range(3)] + [(dve_u, c + 1) for c in range(3)],
            "w2": [(dve_w2, 1)],
        }

        banks_by_name = banks_of(window("tensor"), {kind: len(of) for kind, of in RELEASED.items()})

        def plan(steps, users):
            taken, users = [], dict(users)
            for step in steps:
                mine = []
                for b, readers in zip(banks_by_name[name_of(step)], RELEASED.get(step.kind, [])):
                    mine.append((b, users.get(b, [])))
                    last = Step("norm_attn", step.s, n=step.n) if step.kind == "awo" else step
                    users[b] = [(sig, k, last) for sig, k in zip(readers[::2], readers[1::2])]
                taken.append(mine)
            return taken, users

        def one_round_on(users):
            return {b: [(sig, k, st.moved(-1)) for sig, k, st in u] for b, u in users.items()}

        def rounds_of(engine):
            body = [x for _, x in window(engine)]
            return ([x for x in body if x.n == 0],
                    body,
                    [x for x in body if x.n < 0])

        first_steps, body_steps, last_steps = rounds_of("tensor")
        first_plan, first_users = plan(first_steps, {})
        _, body_users = plan(body_steps, {})
        before = {b: one_round_on(body_users).get(b, []) + one_round_on(first_users).get(b, []) for b in range(BANKS)}
        body_plan, _ = plan(body_steps, before)
        last_plan, _ = plan(last_steps, before)

        def whole_program(eng, engine, run):
            first, body, last = rounds_of(engine)
            run(Round(eng, 0), first)
            with eng.Fori(1, ROUNDS) as i:
                run(Round(eng, i), body)
            run(Round(eng, ROUNDS), last)

        setup_const = room[:, 4 * D:4 * D + NSETUP]
        whole_wqkv = [q_cols[l][:, :, :].rearrange("p c n -> p (c n)")[:, 0:3 * INNER] for l in range(DEPTH)]
        whole_w1 = [room[:, 4 * D + NSETUP + l * 2 * HID:4 * D + NSETUP + (l + 1) * 2 * HID] for l in range(DEPTH)]
        qk_scale = room[:, 4 * D + NSETUP + DEPTH * 2 * HID:4 * D + NSETUP + DEPTH * 2 * (HID + DH)].rearrange(
            "p (l w c) -> p l w c", l=DEPTH, w=2)
        loaded = ctx.enter_context(nc.semaphore("weights_loaded"))
        turned = ctx.enter_context(nc.semaphore("weights_turned"))
        halved = ctx.enter_context(nc.semaphore("weights_halved"))
        LOADS = 2 + 4 + DEPTH * (1 + 1 + 1 + 1 + 1 + 1 + 6 + 2 + 2)

        with nc.Block() as block:
            @block.sync
            def _(sp):
                sp.dma_start(const[:, :], consts[:, 0:NCONST]).then_inc(loaded, 16)
                sp.dma_start(setup_const, consts[:, NCONST:NCONST + NSETUP]).then_inc(loaded, 16)
                for n, w in enumerate((wq, wk, wv, wo_la)):
                    sp.dma_start(room[:, n * D:(n + 1) * D], w).then_inc(loaded, 16)
                for l in range(DEPTH):
                    sp.dma_start(whole_wqkv[l], wqkv[l]).then_inc(loaded, 16)
                    sp.dma_start(wo_sb[:, l, :, :], wo[l].rearrange("(c p) n -> p c n", p=P)).then_inc(loaded, 16)
                    sp.dma_start(whole_w1[l], w1[l]).then_inc(loaded, 16)
                    sp.dma_start(w2_sb[:, l, 0:2, :], w2[l, 0:256, :].rearrange("(c p) n -> p c n", p=P)).then_inc(loaded, 16)
                    sp.dma_start(w2_sb[0:HID - 256, l, 2, :], w2[l, 256:HID, :]).then_inc(loaded, 16)
                    sp.dma_start(b2_rows[:, l, :], b2[l:l + 1, :].to_broadcast([P, D])).then_inc(loaded, 16)
                    for half in range(2):
                        for c, (at, n) in enumerate(HID_CHUNKS):
                            sp.dma_start(b1_cols[0:n, l, half, c:c + 1],
                                         b1[l, half * HID + at:half * HID + at + n].unsqueeze(1)).then_inc(loaded, 16)
                    sp.dma_start(ln_cols[:, l, 0:1], ln_g[l].unsqueeze(1)).then_inc(loaded, 16)
                    sp.dma_start(ln_cols[:, l, 1:2], ln_b[l].unsqueeze(1)).then_inc(loaded, 16)
                    sp.dma_start(qk_scale[:, l, 0, :], q_scale[l:l + 1, :].to_broadcast([P, DH])).then_inc(loaded, 16)
                    sp.dma_start(qk_scale[:, l, 1, :], k_scale[l:l + 1, :].to_broadcast([P, DH])).then_inc(loaded, 16)
                for sig in every:
                    for sem in sig.sems:
                        sp.sem_inc(sem, sig.start())

            @block.gpsimd
            def _(pool):
                for s in range(STREAMS):
                    pool.memset(k_cols[s][:, :, :, :], 0.0)
                    pool.memset(v_rows[s][:, :, :, :], 1.0)
                pool.memset(la_vslot[:, :, :, :], 0.0)
                pool.memset(h_cols[:, :, :], 0.0)
                pool.memset(minus_half[:, :], -0.5)

            @block.tensor
            def _(pe):
                pe.wait_ge(loaded, 16 * LOADS)
                for n in range(4):
                    mm = pe.transpose(bank[0][:, n * D:(n + 1) * D], room[:, n * D:(n + 1) * D], ident)
                mm.then_inc(turned, 1)

            @block.scalar
            def _(act):
                act.wait_ge(loaded, 16 * LOADS)
                for l in range(DEPTH):
                    for whole, halves in ((whole_wqkv[l], wqkv_sb[:, l, :, :]), (whole_w1[l], w1_sb[:, l, :, :])):
                        act.activation(halves[:, 0, :], whole, ACT.Copy, scale=W_SCALE).then_inc(halved, 1)

            @block.vector
            def _(dve):
                dve.wait_ge(loaded, 16 * LOADS)
                for l in range(DEPTH):
                    for c, (_, n) in enumerate(HID_CHUNKS):
                        of = b1_cols[0:n, l, 0, c:c + 1]
                        dve.tensor_scalar(of, of, W_SCALE, None, ALU.mult)
                    for n, (whole, halves) in enumerate(((whole_wqkv[l], wqkv_sb[:, l, :, :]),
                                                         (whole_w1[l], w1_sb[:, l, :, :]))):
                        dve.wait_ge(halved, 2 * l + n + 1)
                        dve.scalar_tensor_tensor(out=halves[:, 1, :], in0=whole, scalar=W_SCALE, in1=halves[:, 0, :],
                                                 op0=ALU.mult, op1=ALU.subtract)
                dve.tensor_copy(ident_h[:, :], ident)
                dve.tensor_copy(mask_h[:, 0, :], cst("mask_first"))
                dve.tensor_copy(mask_h[:, 1, :], cst("mask_later"))
                for l in range(DEPTH):
                    for w, (names, by) in enumerate(((("q_cos", "q_sin"), QK_SCALE), (("k_cos", "k_sin"), 1.0))):
                        sc = qk_scale[:, l, w, :].rearrange("p (a b) -> p a b", a=2)
                        for c, name in enumerate(names):
                            scales = sc[:, ::-1, :] if c else sc
                            for j in range(NT):
                                dve.scalar_tensor_tensor(
                                    out=rope[:, l, 2 * w + c, j * DH:(j + 1) * DH].rearrange("p (a b) -> p a b", a=2),
                                    in0=cst(name)[:, j * DH:(j + 1) * DH].rearrange("p (a b) -> p a b", a=2),
                                    scalar=by, in1=scales, op0=ALU.mult, op1=ALU.mult)
                for s in range(STREAMS):
                    dve.memset(v_even[s][:, 1:NT, :, :], 1.0)
                    dve.memset(v_even[s][0:WIN, 0, :, :], 1.0)
                    dve.memset(v_even[s][WIN:P, 0, :, :], 0.0)
                dve.wait_ge(turned, 1)
                dve.tensor_copy(w_la[:, :], bank[0][:, 0:3 * D])
                dve.tensor_copy(wo_la_t[:, :], bank[0][:, 3 * D:4 * D])

        with nc.Block() as block:
            @block.sync
            def _(sp):
                def load(i, s, n):
                    st = Step("ln_in", s, n=n)
                    sp.wait_ge(*out_stored.at(i, st, back=1, order=0))
                    sp.dma_start(x_io[s][:, :, :], x[bass.ds(i.i * STREAMS + n * STREAMS + s, 1), :, :].rearrange(
                        "o (j p) d -> p (o j) d", p=P)).then_inc(x_loaded.of(st), 16)

                def store(i, s, n):
                    st = Step("ln_out", s, n=n)
                    sp.wait_ge(*dve_out.at(i, st, order=0))
                    sp.dma_start(out[bass.ds(i.i * STREAMS + n * STREAMS + s, 1), :, :].rearrange(
                        "o (j p) d -> p (o j) d", p=P), x_io[s][:, :, :]).then_inc(out_stored.of(st), 16)

                first = Round(sp, 0)
                load(first, 0, 0)
                load(first, 1, 0)
                store(first, 0, 0)
                with sp.Fori(1, ROUNDS) as counter:
                    i = Round(sp, counter)
                    load(i, 0, 0)
                    store(i, 1, -1)
                    load(i, 1, 0)
                    store(i, 0, 0)
                last = Round(sp, ROUNDS)
                store(last, 1, -1)
                for s in range(STREAMS):
                    sp.wait_ge(*out_stored.at(last, Step("ln_out", s, n=-1), order=0))

            @block.tensor
            def _(pe):
                def take(i, banks, use):
                    b, users = banks[use]
                    for sig, k, st in users:
                        pe.wait_ge(*sig.at(i, st, k, order=0 if sig.steps == 1 else None))
                    return bank[b]

                def yt(i, st, banks):
                    to = take(i, banks, 0)
                    pe.wait_ge(*dve_ln.at(i, Step("ln_in", st.s, n=st.n)))
                    for j in range(NT):
                        mm = pe.transpose(to[:, j * P:(j + 1) * P], y_rows[:, j, :], ident)
                    mm.then_inc(pe_yt.of(st), 1)

                def aqkv(i, st, banks):
                    to = take(i, banks, 0)
                    pe.wait_ge(*act_yt.at(i, Step("yt", st.s, n=st.n)))
                    pe.matmul(to[:, 0:3 * D], y_cols[:, st.j * P:(st.j + 1) * P], w_la[:, :],
                              start=True, stop=True).then_inc(pe_aqkv.of(st), 1)

                def at(i, st, banks):
                    to = take(i, banks, 0)
                    pe.wait_ge(*dve_aphi.at(i, Step("aqkv", st.s, 0, st.j, st.n)))
                    for w in range(2):
                        mm = pe.transpose(to[:, w * P:(w + 1) * P], la_phi[:, st.j, w * D:(w + 1) * D], ident)
                    mm.then_inc(pe_at.of(st), 1)

                def scores_linear(i, st, banks):
                    a = st.j % 2
                    pe.wait_ge(*pool_qexp.at(i, Step("at", st.s, 0, st.j, st.n)))
                    for g in range(GROUPS):
                        to = take(i, banks, g)
                        rows = slice(32 * g, 32 * g + 32)
                        pe.matmul(to[:, :], la_qk_cols[rows, a, P:2 * P],
                                  la_qexp[rows, a, :, :].rearrange("p s q -> p (s q)"),
                                  start=True, stop=True).then_inc(pe_as.of(st), 1)

                def out_linear(i, st, banks):
                    j, a = st.j, st.j % 2
                    to = take(i, banks, 0)
                    pe.wait_ge(*act_av.at(i, Step("aqkv", st.s, 0, j, st.n)))
                    q_tile = la_qk_cols[:, a, 0:P]
                    started = False
                    if j < NT - 1:
                        pe.matmul(to[:, 256:384], la_phi[:, j, D:2 * D], la_v[:, j, :], start=True, stop=True,
                                  skip_group_check=True)
                        pe.matmul(to[:, 384:512], la_phi[:, j, D:2 * D], cst("ones").to_broadcast([P, D]), start=False, stop=True,
                                  skip_group_check=True)
                        started = True
                    if j > 0:
                        pe.wait_ge(*dve_state.at(i, st, order=j - 1))
                        pe.matmul(to[:, 0:P], la_state[st.s][:, 0:D], q_tile, start=not started, stop=False,
                                  skip_group_check=True)
                        pe.matmul(to[:, P:2 * P], la_state[st.s][:, D:2 * D], q_tile, start=False, stop=False,
                                  skip_group_check=True)
                    pe.wait_ge(*act_slots.at(i, Step("as", st.s, 0, j, st.n)))
                    for g in range(GROUPS):
                        pe.wait_ge(*dve_sm.at(i, Step("as", st.s, 0, j, st.n), g + 1))
                        for sl in range(SLOTS):
                            mm = pe.matmul(to[32 * g:32 * g + 32, 0:P], la_vslot[:, a, g * SLOTS + sl, :],
                                           la_sm[:, a, g, sl, :], start=False, stop=(sl == SLOTS - 1), skip_group_check=True)
                            mm = pe.matmul(to[32 * g:32 * g + 32, P:2 * P],
                                           cst("ones_slot")[:, sl * 32:(sl + 1) * 32],
                                           la_sm[:, a, g, sl, :], start=False, stop=(sl == SLOTS - 1),
                                           skip_group_check=True)
                    mm.then_inc(pe_ao.of(st), 1)

                def awo(i, st, banks):
                    to = take(i, banks, 0)
                    for j in range(NT):
                        pe.wait_ge(*dve_ao.at(i, Step("ao", st.s, 0, j, st.n)))
                        mm = pe.matmul(to[:, j * D:(j + 1) * D], y_cols[:, j * P:(j + 1) * P], wo_la_t[:, :],
                                       start=True, stop=True)
                    mm.then_inc(pe_awo.of(st), 1)

                def h(i, st, banks):
                    to = take(i, banks, 0)
                    if st.l == 0:
                        pe.wait_ge(*dve_ln.at(i, Step("ln_mid", st.s, n=st.n)))
                    else:
                        pe.wait_ge(*dve_w2.at(i, Step("w2", st.s, st.l - 1, 0, st.n)))
                    for j in range(NT):
                        mm = pe.transpose(to[:, j * P:(j + 1) * P], x_res[st.s][:, j, :], ident)
                    mm.then_inc(pe_h.of(st), 1)

                def qkv(i, st, banks):
                    pe.wait_ge(*act_h.at(i, Step("h", st.s, st.l, 0, st.n)))
                    for w in range(3):
                        to = take(i, banks, w)
                        for n, (x_half, w_half) in enumerate(PASSES):
                            if x_half == 1 and w == 0:
                                pe.wait_ge(*dve_h.at(i, Step("h", st.s, st.l, 0, st.n)))
                            mm = pe.matmul(to[:, :], h_cols[:, x_half, st.j * P:(st.j + 1) * P],
                                           wqkv_sb[:, st.l, w_half, w * INNER:(w + 1) * INNER],
                                           start=(n == 0), stop=(n == 2))
                        mm.then_inc(pe_qkv.of(st), 1)

                def qkt(i, st, banks):
                    a = st.j % 2
                    qkv_step = Step("qkv", st.s, st.l, st.j, st.n)
                    for n, w in enumerate((1, 0)):
                        to = take(i, banks, n)
                        pe.wait_ge(*pool_qk.at(i, qkv_step, 1 + n))
                        for c in range(PAIRS):
                            mm = pe.transpose(to[:, c * P:(c + 1) * P], qk_t[:, a, w, 0, c * P:(c + 1) * P], ident)
                        mm.then_inc(pe_qkt.of(st), 1)

                def scores(i, st, banks):
                    j, g = st.j // 2, st.j % 2
                    to = take(i, banks, 0)
                    tile = Step("qkt", st.s, st.l, j, st.n)
                    if g == 0:
                        pe.wait_ge(*act_q.at(i, tile))
                        pe.wait_ge(*dve_k.at(i, tile))
                        pe.wait_ge(*act_k.at(i, tile))
                    pe.matmul(to[:, :], ident_h[:, :], mask_h[:, min(j, 1), :], start=True, stop=False,
                              skip_group_check=True)
                    for c in range(2):
                        pair = 2 * g + c
                        for w in range(2):
                            first = j * WIN
                            keys = k_windows(k_cols[st.s][:, pair, :, :], w * WIN, first)
                            mm = pe.matmul(to[w * WIN:(w + 1) * WIN, c * 256:(c + 1) * 256],
                                           q_cols[st.s][:, pair, j * P + w * WIN:j * P + (w + 1) * WIN], keys,
                                           start=False, stop=True, skip_group_check=True)
                    mm.then_inc(pe_s.of(st), 1)

                def turn_probs(i, st, banks):
                    to = take(i, banks, 0)
                    pe.wait_ge(*act_p.at(i, Step("s", st.s, st.l, st.j, st.n)))
                    for n in range(4):
                        mm = pe.transpose(to[:, n * P:(n + 1) * P], probs[:, st.j % 3, n * P:(n + 1) * P], ident)
                    mm.then_inc(pe_pt.of(st), 1)

                def mix(i, st, banks):
                    j, g = st.j // 2, st.j % 2
                    to = take(i, banks, 0)
                    tile = Step("qkv", st.s, st.l, j, st.n)
                    if g == 0:
                        pe.wait_ge(*act_qkv.at(i, tile))
                    pe.wait_ge(*act_pt.at(i, Step("pt", st.s, st.l, st.j, st.n)))
                    for n in range(4):
                        for w in range(2):
                            values = (v_even if w == 0 else v_rows)[st.s]
                            mm = pe.matmul(to[w * WIN:(w + 1) * WIN, n * VW:(n + 1) * VW],
                                           probs_t[:, st.j % 2, n * P + w * WIN:n * P + (w + 1) * WIN],
                                           values[:, j, 4 * g + n, :], start=True, stop=True)
                    mm.then_inc(pe_o.of(st), 1)

                def turn_out(i, st, banks):
                    to = take(i, banks, 0)
                    pe.wait_ge(*dve_on.at(i, Step("o", st.s, st.l, 2 * st.j + 1, st.n)))
                    for c in range(PAIRS):
                        mm = pe.transpose(to[:, c * P:(c + 1) * P], o_rows[:, c * P:(c + 1) * P], ident)
                    mm.then_inc(pe_ot.of(st), 1)

                def project(i, st, banks):
                    to = take(i, banks, 0)
                    pe.wait_ge(*act_ot.at(i, Step("ot", st.s, st.l, st.j, st.n)))
                    for c in range(PAIRS):
                        mm = pe.matmul(to[:, 0:D], o_cols[:, c * P:(c + 1) * P], wo_sb[:, st.l, c, :],
                                       start=(c == 0), stop=(c == PAIRS - 1))
                    mm.then_inc(pe_wo.of(st), 1)

                def shift(i, st, banks):
                    to = take(i, banks, 0)
                    pe.wait_ge(*dve_wo.at(i, Step("wo", st.s, st.l, NT - 1, st.n)))
                    pe.matmul(to[:, 0:NT * DH], cst("shift"), x_res[st.s][:, :, DH:D], start=True, stop=True)
                    pe.matmul(to[:, DH:NT * DH], cst("wrap"), x_res[st.s][:, 0:NT - 1, DH:D],
                              start=False, stop=True, skip_group_check=True).then_inc(pe_sh.of(st), 1)

                def h2t(i, st, banks):
                    to = take(i, banks, 0)
                    pe.wait_ge(*dve_ln.at(i, Step("ln_ffn", st.s, st.l, 0, st.n)))
                    for j in range(NT):
                        mm = pe.transpose(to[:, j * P:(j + 1) * P], h2_rows[:, j, :], ident)
                    mm.then_inc(pe_h2t.of(st), 1)

                def up(i, st, banks):
                    pe.wait_ge(*act_h2t.at(i, Step("h2t", st.s, st.l, 0, st.n), 1))
                    for half in (1, 0):
                        for c, (at_, n) in enumerate(HID_CHUNKS):
                            to = take(i, banks, c + 3 * (1 - half))
                            for p, (x_half, w_half) in enumerate(PASSES):
                                if x_half == 1 and half == 1 and c == 0:
                                    pe.wait_ge(*dve_h2t.at(i, Step("h2t", st.s, st.l, 0, st.n)))
                                mm = pe.matmul(to[0:n, :], w1_sb[:, st.l, w_half, half * HID + at_:half * HID + at_ + n],
                                               h2_cols[:, x_half, :], start=(p == 0), stop=(p == 2))
                            mm.then_inc(pe_w1.of(st), 1)

                def down(i, st, banks):
                    to = take(i, banks, 0)
                    for c in range(3):
                        pe.wait_ge(*dve_u.at(i, Step("w1", st.s, st.l, 0, st.n), c + 1))
                    for j in range(NT):
                        for c, (_, n) in enumerate(HID_CHUNKS):
                            mm = pe.matmul(to[:, j * D:(j + 1) * D], hidden[0:n, c, j * P:(j + 1) * P],
                                           w2_sb[0:n, st.l, c, :], start=(c == 0), stop=(c == 2))
                    mm.then_inc(pe_w2.of(st), 1)

                does = {"yt": yt, "aqkv": aqkv, "at": at, "as": scores_linear, "ao": out_linear, "awo": awo, "h": h,
                        "qkv": qkv, "qkt": qkt, "s": scores, "pt": turn_probs, "o": mix, "ot": turn_out,
                        "wo": project, "sh": shift, "h2t": h2t, "w1": up, "w2": down}

                def run(i, steps, planned):
                    for st, banks in zip(steps, planned):
                        if st.kind in does:
                            does[st.kind](i, st, banks)

                run(Round(pe, 0), first_steps, first_plan)
                with pe.Fori(1, ROUNDS) as i:
                    run(Round(pe, i), body_steps, body_plan)
                run(Round(pe, ROUNDS), last_steps, last_plan)

            @block.scalar
            def _(act):
                def copy(to, of):
                    return act.activation(to, of, ACT.Copy)

                def scaled(to, of):
                    return act.activation(to, of, ACT.Copy, scale=1 / W_SCALE)

                def yt(i, st, b):
                    act.wait_ge(*pe_yt.at(i, st))
                    copy(y_cols[:, :], bank[b[0]][:, :]).then_inc(act_yt.of(st), 1)

                def aqkv(i, st, b):
                    act.wait_ge(*pe_aqkv.at(i, st))
                    copy(la_v[:, st.j, :], bank[b[0]][:, 2 * D:3 * D]).then_inc(act_av.of(st), 1)

                def slots_linear(i, st, b):
                    slots = la_vslot[:, st.j % 2, :, :].rearrange("p (g s) w -> p g (s w)", g=GROUPS)
                    values = la_v[:, st.j, :].rearrange("p (g s e) -> p g s e", g=GROUPS, s=SLOTS)
                    act.wait_ge(*act_av.at(i, Step("aqkv", st.s, 0, st.j, st.n)))
                    act.wait_ge(*pe_ao.at(i, Step("ao", st.s, 0, st.j, st.n), back=2))
                    for sl in range(SLOTS):
                        ins = copy(slots[:, :, sl * 32 + sl * LA_DH:sl * 32 + (sl + 1) * LA_DH],
                                   values[:, :, sl, :])
                    ins.then_inc(act_slots.of(st), 1)

                def exp_linear(i, st, b):
                    a = st.j % 2
                    act.wait_ge(*pool_ar.at(i, st))
                    act.activation(la_tb[:, a, :], la_ta[:, a, :], ACT.Exp).then_inc(act_aexp.of(st), 1)

                def at(i, st, b):
                    act.wait_ge(*pe_at.at(i, st))
                    act.wait_ge(*pe_ao.at(i, Step("ao", st.s, 0, st.j, st.n), back=2))
                    copy(la_qk_cols[:, st.j % 2, :], bank[b[0]][:, 0:2 * P]).then_inc(act_at.of(st), 1)

                def h(i, st, b):
                    act.wait_ge(*pe_h.at(i, st))
                    copy(h_cols[0:DH, 0, :], bank[b[0]][0:DH, :]).then_inc(act_h.of(st), 1)
                    copy(h_cols[DH:P, 0, 1:T], bank[b[0]][DH:P, 0:T - 1]).then_inc(act_h.of(st), 1)

                def qkv(i, st, b):
                    a = st.j % 2
                    act.wait_ge(*dve_ss.at(i, st, 1, back=1))
                    for w in range(2):
                        act.wait_ge(*pe_qkv.at(i, st, w + 1))
                        act.activation(qk_sq[:, w * INNER:(w + 1) * INNER], bank[b[w]][:, :],
                                       ACT.Square).then_inc(act_qkv.of(st), 1)
                    act.wait_ge(*pe_qkv.at(i, st, 3))
                    values = bank[b[2]][:, :].rearrange("p (h d) -> p h d", h=HEADS)
                    scaled(v_rows[st.s][:, st.j, :, 0:DH], values).then_inc(act_qkv.of(st), 1)
                    if st.j < NT - 1:
                        scaled(v_even[st.s][0:WIN, st.j, :, 0:DH], values[0:WIN]).then_inc(act_qkv.of(st), 1)
                        scaled(v_even[st.s][WIN:P, st.j + 1, :, 0:DH], values[WIN:P]).then_inc(act_qkv.of(st), 1)
                    else:
                        for heads in (slice(0, 4), slice(4, 8)):
                            scaled(v_even[st.s][0:WIN, st.j, heads, 0:DH],
                                   values[0:WIN, heads, :]).then_inc(act_qkv.of(st), 1)

                def qkt(i, st, b):
                    act.wait_ge(*pe_qkt.at(i, st, 1))
                    turned_keys(copy, st, b, 1).then_inc(act_k.of(st), 1)
                    act.wait_ge(*pe_qkt.at(i, st, 2))
                    copy(q_cols[st.s][:, :, st.j * P:(st.j + 1) * P],
                         bank[b[1]][:, :].rearrange("p (c n) -> p c n", c=PAIRS)).then_inc(act_q.of(st), 1)

                def exps(i, st, b):
                    j, g = st.j // 2, st.j % 2
                    act.wait_ge(*dve_max.at(i, st))
                    act.wait_ge(*pe_pt.at(i, st, back=3))
                    for n in range(4):
                        act.activation(probs[:, st.j % 3, n * P:(n + 1) * P], bank[b[0]][:, n * P:(n + 1) * P], ACT.Exp,
                                       bias=s_bias[st.s][:, st.j, n:n + 1],
                                       scale=qk_rnorm[st.s][:, j, 4 * g + n:4 * g + n + 1]).then_inc(act_p.of(st), 1)

                def probs_turned(i, st, b):
                    act.wait_ge(*pe_pt.at(i, st))
                    act.wait_ge(*pe_o.at(i, st, back=2))
                    copy(probs_t[:, st.j % 2, :], bank[b[0]][:, :]).then_inc(act_pt.of(st), 1)

                def out_turned(i, st, b):
                    act.wait_ge(*pe_ot.at(i, st))
                    act.wait_ge(*pe_wo.at(i, st, back=1))
                    copy(o_cols[:, :], bank[b[0]][:, :]).then_inc(act_ot.of(st), 1)

                def shifted(i, st, b):
                    act.wait_ge(*dve_wo.at(i, Step("wo", st.s, st.l, NT - 1, st.n)))
                    copy(h2_rows[:, :, 0:DH], x_res[st.s][:, :, 0:DH]).then_inc(act_h2x.of(st), 1)

                def h2t(i, st, b):
                    act.wait_ge(*pe_h2t.at(i, st))
                    for to in (h2_cols[:, 0, :], h2_whole):
                        act.activation(to, bank[b[0]][:, :], ACT.Identity, bias=ln_cols[:, st.l, 1:2],
                                       scale=ln_cols[:, st.l, 0:1]).then_inc(act_h2t.of(st), 1)

                def gelus(i, st, b):
                    for c, (_, n) in enumerate(HID_CHUNKS):
                        act.wait_ge(*pe_w1.at(i, st, c + 1))
                        act.activation(hidden[0:n, c, :], bank[b[c]][0:n, :], ACT.Gelu, scale=1 / W_SCALE,
                                       bias=b1_cols[0:n, st.l, 1, c:c + 1]).then_inc(act_gelu.of(st), 1)

                does = {"yt": yt, "aqkv": aqkv, "phi": exp_linear, "at": at, "as": slots_linear, "h": h, "qkv": qkv, "qkt": qkt, "s": exps,
                        "pt": probs_turned, "ot": out_turned, "sh": shifted, "h2t": h2t, "w1": gelus}

                def run(i, steps):
                    for st in steps:
                        if st.kind in does:
                            does[st.kind](i, st, banks_by_name[name_of(st)])

                whole_program(act, "scalar", run)

            @block.vector
            def _(dve):
                def stats(i, st, of):
                    s, o = st.s, order_of(st)
                    for j in range(NT):
                        dve.bn_stats(ln_stats[s][:, o, j, :], of(j)).then_inc(dve_ln.of(st), 1)
                    dve.wait_ge(*dve_ln.at(i, st, 4))
                    dve.memset(ln_held[s][:, o:o + 1], 0.0)
                    for j in range(NT):
                        dve.bn_aggr(ln_mv[s][:, o, j, :], ln_stats[s][:, o, j, :]).then_inc(dve_ln.of(st), 1)
                    dve.wait_ge(*dve_ln.at(i, st, 8))
                    dve.tensor_scalar(ln_var[s][:, o, :], ln_mv[s][:, o, :, 1], LN_EPS, None,
                                      ALU.add).then_inc(dve_ln.of(st), 1)

                def normed(i, st, of, to):
                    s, o = st.s, order_of(st)
                    dve.wait_ge(*pool_rstd.at(i, st))
                    for j in range(NT):
                        dve.tensor_scalar(to(j), of(j), ln_mv[s][:, o, j, 0:1], ln_rstd[s][:, o, j:j + 1],
                                          ALU.subtract, ALU.mult).then_inc(dve_ln.of(st), 1)

                def ln_in(i, st, b):
                    dve.wait_ge(*x_loaded.at(i, st, order=0))
                    stats(i, st, lambda j: x_io[st.s][:, j, :])

                def norm_in(i, st, b):
                    normed(i, st, lambda j: x_io[st.s][:, j, :], lambda j: y_rows[:, j, :])

                def ln_attn(i, st, b):
                    dve.wait_ge(*pe_awo.at(i, Step("awo", st.s, n=st.n)))
                    stats(i, st, lambda j: bank[b[0]][:, j * D:(j + 1) * D])

                def norm_attn(i, st, b):
                    normed(i, st, lambda j: bank[b[0]][:, j * D:(j + 1) * D], lambda j: y_rows[:, j, :])
                    dve.wait_ge(*dve_ln.at(i, st))
                    dve.tensor_tensor(x_io[st.s][:, :, :], x_io[st.s][:, :, :], y_rows[:, :, :],
                                      ALU.add).then_inc(dve_xmid.of(st), 1)

                def ln_mid(i, st, b):
                    dve.wait_ge(*dve_xmid.at(i, st, order=0))
                    stats(i, st, lambda j: x_io[st.s][:, j, :])

                def norm_mid(i, st, b):
                    normed(i, st, lambda j: x_io[st.s][:, j, :], lambda j: x_res[st.s][:, j, :])

                def ln_ffn(i, st, b):
                    sh = Step("sh", st.s, st.l, 0, st.n)
                    dve.wait_ge(*dve_h2.at(i, sh))
                    dve.wait_ge(*act_h2x.at(i, sh))
                    stats(i, st, lambda j: h2_rows[:, j, :])

                def norm_ffn(i, st, b):
                    normed(i, st, lambda j: h2_rows[:, j, :], lambda j: h2_rows[:, j, :])

                def ln_out(i, st, b):
                    dve.wait_ge(*dve_w2.at(i, Step("w2", st.s, DEPTH - 1, 0, st.n)))
                    stats(i, st, lambda j: x_res[st.s][:, j, :])

                def norm_out(i, st, b):
                    normed(i, st, lambda j: x_res[st.s][:, j, :], lambda j: x_res[st.s][:, j, :])
                    dve.wait_ge(*dve_ln.at(i, st))
                    dve.tensor_tensor(x_io[st.s][:, :, :], x_res[st.s][:, :, :], x_io[st.s][:, :, :],
                                      ALU.add).then_inc(dve_out.of(st), 1)

                def rope_linear(i, st, b):
                    a, j = st.j % 2, st.j
                    qk = bank[b[0]][:, 0:2 * D]
                    cos = cst("la_cos")[:, j * LA_DH:(j + 1) * LA_DH]
                    sin = cst("la_sin")[:, j * LA_DH:(j + 1) * LA_DH].rearrange("p (t c) -> p t c", t=2)
                    dve.wait_ge(*act_av.at(i, st))
                    dve.wait_ge(*pool_ar.at(i, st, 1, back=2))
                    dve.wait_ge(*dve_aphi.at(i, st, back=2))
                    dve.tensor_tensor(la_ta[:, a, :].rearrange("p (h c) -> p h c", c=LA_DH),
                                      qk.rearrange("p (h c) -> p h c", c=LA_DH),
                                      cos.unsqueeze(1).to_broadcast([P, 2 * LA_HEADS, LA_DH]),
                                      ALU.mult).then_inc(dve_arope.of(st), 1)
                    dve.tensor_tensor(
                        la_tb[:, a, :].rearrange("p (h t c) -> p h t c", t=2, c=LA_DH // 2),
                        qk.rearrange("p (h t c) -> p h t c", t=2, c=LA_DH // 2)[:, :, ::-1, :],
                        sin.unsqueeze(1).to_broadcast([P, 2 * LA_HEADS, 2, LA_DH // 2]),
                        ALU.mult).then_inc(dve_arope.of(st), 1)

                def phi_linear(i, st, b):
                    a = st.j % 2
                    dve.wait_ge(*pool_ar.at(i, st))
                    dve.tensor_scalar(la_phi[:, st.j, :], la_ta[:, a, :], 0.0, None, ALU.max).then_inc(dve_aphi.of(st), 1)
                    dve.wait_ge(*act_aexp.at(i, st))
                    dve.wait_ge(*dve_aphi.at(i, st, 1))
                    dve.scalar_tensor_tensor(out=la_phi[:, st.j, :], in0=la_tb[:, a, :], scalar=1.0,
                                             in1=la_phi[:, st.j, :], op0=ALU.min, op1=ALU.add).then_inc(dve_aphi.of(st), 1)

                def mask_linear(i, st, b):
                    a = st.j % 2
                    dve.wait_ge(*pe_ao.at(i, Step("ao", st.s, 0, st.j, st.n), back=2))
                    for g in range(GROUPS):
                        dve.wait_ge(*pe_as.at(i, st, g + 1))
                        dve.tensor_tensor(la_sm[:, a, g, :, :],
                                          bank[b[g]][:, :].rearrange("p (s q) -> p s q", s=SLOTS),
                                          cst("causal").unsqueeze(1).to_broadcast([P, SLOTS, P]),
                                          ALU.mult).then_inc(dve_sm.of(st), 1)

                def out_linear(i, st, b):
                    s, j, of = st.s, st.j, bank[b[0]]
                    dve.wait_ge(*pe_ao.at(i, st))
                    if j < NT - 1:
                        dve.wait_ge(*dve_state.at(i, st, back=1, order=j))
                        dve.tensor_tensor(la_tmp[:, :], of[:, 256:512], cst("block"),
                                          ALU.mult).then_inc(dve_state.of(st), 1)
                        dve.wait_ge(*dve_state.at(i, st, 1, order=j))
                        dve.tensor_tensor(la_state[s][:, :], la_tmp[:, :],
                                          cst("zeros").to_broadcast([P, 2 * D]) if j == 0 else la_state[s][:, :],
                                          ALU.add).then_inc(dve_state.of(st), 1)
                    dve.wait_ge(*dve_ao.at(i, st, back=1))
                    dve.tensor_scalar(la_den[:, :], of[:, P:2 * P], DEN_EPS, None, ALU.max).then_inc(dve_ao.of(st), 1)
                    dve.wait_ge(*dve_ao.at(i, st, 1))
                    dve.reciprocal(la_den[:, :], la_den[:, :]).then_inc(dve_ao.of(st), 1)
                    dve.wait_ge(*dve_ao.at(i, st, 2))
                    dve.tensor_tensor(y_cols[:, j * P:(j + 1) * P], of[:, 0:P], la_den[:, :],
                                      ALU.mult).then_inc(dve_ao.of(st), 1)

                def lower_h(i, st, b):
                    dve.wait_ge(*act_h.at(i, st))
                    dve.tensor_tensor(h_cols[0:DH, 1, :], bank[b[0]][0:DH, :], h_cols[0:DH, 0, :],
                                      ALU.subtract).then_inc(dve_h.of(st), 1)
                    dve.tensor_tensor(h_cols[DH:P, 1, 1:T], bank[b[0]][DH:P, 0:T - 1], h_cols[DH:P, 0, 1:T],
                                      ALU.subtract).then_inc(dve_h.of(st), 1)

                def lower_h2(i, st, b):
                    dve.wait_ge(*act_h2t.at(i, st))
                    dve.tensor_tensor(h2_cols[:, 1, :], h2_whole, h2_cols[:, 0, :],
                                      ALU.subtract).then_inc(dve_h2t.of(st), 1)

                def rope_softmax(i, st, b):
                    s, l, j, a = st.s, st.l, st.j, st.j % 2
                    dve.wait_ge(*pe_qkt.at(i, Step("qkt", s, l, j, st.n), back=2))
                    dve.wait_ge(*act_qkv.at(i, st, 2))
                    dve.wait_ge(*pool_rnorm.at(i, st, back=NT))
                    dve.tensor_reduce(qk_ss[s][:, j, :], qk_sq.rearrange("p (h c) -> p h c", c=DH), AX.X,
                                      ALU.add).then_inc(dve_ss.of(st), 1)
                    dve.wait_ge(*dve_ss.at(i, st, 1))
                    dve.tensor_scalar(qk_ss[s][:, j, :], qk_ss[s][:, j, :], (NORM_EPS * W_SCALE) ** 2, None,
                                      ALU.max).then_inc(dve_ss.of(st), 1)
                    for w in (1, 0):
                        of = bank[b[w]][:, :]
                        cos = rope[:, l, 2 * w, j * DH:(j + 1) * DH]
                        sin = rope[:, l, 2 * w + 1, j * DH:(j + 1) * DH].rearrange("p (t c) -> p t c", t=2)
                        dve.tensor_tensor(qk_t[:, a, w, 0, :].rearrange("p (h c) -> p h c", c=DH),
                                          of.rearrange("p (h c) -> p h c", c=DH),
                                          cos.unsqueeze(1).to_broadcast([P, HEADS, DH]),
                                          ALU.mult).then_inc(dve_rope.of(st), 1)
                        dve.tensor_tensor(
                            qk_t[:, a, w, 1, :].rearrange("p (h t c) -> p h t c", t=2, c=DH // 2),
                            of.rearrange("p (h t c) -> p h t c", t=2, c=DH // 2)[:, :, ::-1, :],
                            sin.unsqueeze(1).to_broadcast([P, HEADS, 2, DH // 2]),
                            ALU.mult).then_inc(dve_rope.of(st), 1)
                    dve.wait_ge(*dve_rope.at(i, st, 2))
                    dve.tensor_tensor(qk_t[:, a, 1, 0, :], qk_t[:, a, 1, 0, :], qk_t[:, a, 1, 1, :],
                                      ALU.add).then_inc(dve_k_rotated.of(st), 1)

                def keys_turned(i, st, b):
                    dve.wait_ge(*pe_qkt.at(i, st, 1))
                    turned_keys(dve.tensor_copy, st, b, 0).then_inc(dve_k.of(st), 1)

                def maxima(i, st, b):
                    j, g = st.j // 2, st.j % 2
                    dve.wait_ge(*pe_s.at(i, st))
                    dve.wait_ge(*act_p.at(i, st, back=UNITS))
                    dve.wait_ge(*dve_max.at(i, st, back=UNITS))
                    dve.tensor_reduce(s_max[st.s][:, st.j, :], bank[b[0]][:, :].rearrange("p (h k) -> p h k", h=4), AX.X,
                                      ALU.max).then_inc(dve_max.of(st), 1)
                    if g == 0:
                        dve.wait_ge(*pool_rnorm.at(i, Step("qkv", st.s, st.l, j, st.n)))
                    dve.wait_ge(*dve_max.at(i, st, 1))
                    dve.scalar_tensor_tensor(out=s_bias[st.s][:, st.j, :], in0=s_max[st.s][:, st.j, :], scalar=-1.0,
                                             in1=qk_rnorm[st.s][:, j, 4 * g:4 * g + 4], op0=ALU.mult,
                                             op1=ALU.mult).then_inc(dve_max.of(st), 1)

                def divide(i, st, b):
                    j, g = st.j // 2, st.j % 2
                    of = bank[b[0]][:, 0:4 * VW].rearrange("p (h c) -> p h c", c=VW)
                    dve.wait_ge(*pe_o.at(i, st))
                    dve.wait_ge(*dve_on.at(i, st, back=UNITS))
                    dve.reciprocal(o_rden[st.s][:, st.j, :], of[:, :, DH]).then_inc(dve_on.of(st), 1)
                    if g == 0:
                        dve.wait_ge(*pe_ot.at(i, Step("ot", st.s, st.l, j, st.n), back=1))
                    dve.wait_ge(*dve_on.at(i, st, 1))
                    dve.tensor_tensor(
                        o_rows[:, g * 256:(g + 1) * 256].rearrange("p (h c) -> p h c", c=DH), of[:, :, 0:DH],
                        o_rden[st.s][:, st.j, :].unsqueeze(2).to_broadcast([P, 4, DH]), ALU.mult).then_inc(dve_on.of(st), 1)

                def add_attention(i, st, b):
                    x_tile = x_res[st.s][:, st.j, :]
                    dve.wait_ge(*pe_wo.at(i, st))
                    dve.tensor_tensor(x_tile, x_tile, bank[b[0]][:, 0:D], ALU.add).then_inc(dve_wo.of(st), 1)

                def shifted(i, st, b):
                    dve.wait_ge(*pe_sh.at(i, st))
                    dve.tensor_copy(h2_rows[:, :, DH:D], bank[b[0]][:, 0:NT * DH].rearrange(
                        "p (j c) -> p j c", j=NT)).then_inc(dve_h2.of(st), 1)

                def gate(i, st, b):
                    for c, (_, n) in enumerate(HID_CHUNKS):
                        dve.wait_ge(*pe_w1.at(i, st, 4 + c))
                        dve.wait_ge(*act_gelu.at(i, st, c + 1))
                        dve.scalar_tensor_tensor(out=hidden[0:n, c, :], in0=bank[b[3 + c]][0:n, :],
                                                 scalar=b1_cols[0:n, st.l, 0, c:c + 1], in1=hidden[0:n, c, :],
                                                 op0=ALU.add, op1=ALU.mult).then_inc(dve_u.of(st), 1)

                def add_ffn(i, st, b):
                    x_all = x_res[st.s][:, :, :]
                    dve.wait_ge(*pe_w2.at(i, st))
                    dve.wait_ge(*pool_b2.at(i, Step("sh", st.s, st.l, 0, st.n)))
                    dve.scalar_tensor_tensor(out=x_all, in0=bank[b[0]][:, :].rearrange("p (j c) -> p j c", j=NT),
                                             scalar=1 / W_SCALE, in1=x_all, op0=ALU.mult,
                                             op1=ALU.add).then_inc(dve_w2.of(st), 1)

                does = {"ln_in": ln_in, "ln_attn": ln_attn, "ln_mid": ln_mid, "ln_ffn": ln_ffn, "ln_out": ln_out,
                        "norm_in": norm_in, "norm_attn": norm_attn, "norm_mid": norm_mid, "norm_ffn": norm_ffn,
                        "norm_out": norm_out, "phi": phi_linear, "h": lower_h, "h2t": lower_h2,
                        "aqkv": rope_linear, "as": mask_linear, "ao": out_linear, "qkv": rope_softmax,
                        "qkt": keys_turned, "s": maxima, "o": divide, "wo": add_attention, "sh": shifted,
                        "w1": gate, "w2": add_ffn}

                def run(i, steps):
                    for st in steps:
                        if st.kind in does:
                            of = Step("awo", st.s) if st.kind in ("ln_attn", "norm_attn") else st
                            does[st.kind](i, st, banks_by_name[name_of(of)])

                whole_program(dve, "vector", run)

            @block.gpsimd
            def _(pool):
                def rstd(i, st):
                    s, o = st.s, order_of(st)
                    pool.wait_ge(*dve_ln.at(i, st, 9))
                    pool.tensor_tensor(ln_rstd[s][:, o, :], ln_var[s][:, o, :], minus_half[:, 0:NT],
                                       ALU.pow).then_inc(pool_rstd.of(st), 1)

                def rotate_linear(i, st):
                    a = st.j % 2
                    pool.wait_ge(*dve_arope.at(i, st))
                    pool.tensor_tensor(la_ta[:, a, :], la_ta[:, a, :], la_tb[:, a, :],
                                       ALU.add).then_inc(pool_ar.of(st), 1)

                def expand(i, st):
                    a = st.j % 2
                    pool.wait_ge(*act_at.at(i, st))
                    pool.wait_ge(*pe_as.at(i, Step("as", st.s, 0, st.j, st.n), back=2))
                    pool.tensor_tensor(la_qexp[:, a, :, :],
                                      la_qk_cols[:, a, 0:P].unsqueeze(1).to_broadcast([P, SLOTS, P]),
                                      cst("slot").unsqueeze(2).to_broadcast([P, SLOTS, P]),
                                      ALU.mult).then_inc(pool_qexp.of(st), 1)

                def rotate_softmax(i, st):
                    s, j, a = st.s, st.j, st.j % 2
                    heads = lambda t: t.rearrange("p (h c) -> p h c", c=DH)
                    def inverse_norms(heads_of):
                        pool.tensor_tensor(qk_rnorm[s][:, j, heads_of], qk_ss[s][:, j, heads_of], minus_half[:, heads_of],
                                           ALU.pow).then_inc(pool_rnorm.of(st), 1)

                    pool.wait_ge(*dve_ss.at(i, st))
                    inverse_norms(slice(HEADS, 2 * HEADS))
                    pool.wait_ge(*pool_rnorm.at(i, st, 1))
                    pool.wait_ge(*dve_k_rotated.at(i, st))
                    pool.tensor_tensor(heads(qk_t[:, a, 1, 0, :]), heads(qk_t[:, a, 1, 0, :]),
                                       qk_rnorm[s][:, j, HEADS:2 * HEADS].unsqueeze(2).to_broadcast([P, HEADS, DH]),
                                       ALU.mult).then_inc(pool_qk.of(st), 1)
                    pool.wait_ge(*dve_rope.at(i, st, 4))
                    pool.tensor_tensor(qk_t[:, a, 0, 0, :], qk_t[:, a, 0, 0, :], qk_t[:, a, 0, 1, :],
                                       ALU.add).then_inc(pool_qk.of(st), 1)
                    inverse_norms(slice(0, HEADS))

                def bias(i, st):
                    x_all = x_res[st.s][:, :, :]
                    pool.wait_ge(*pe_sh.at(i, st))
                    pool.wait_ge(*act_h2x.at(i, st))
                    pool.tensor_tensor(x_all, x_all, b2_rows[:, st.l, :].unsqueeze(1).to_broadcast([P, NT, D]),
                                       ALU.add).then_inc(pool_b2.of(st), 1)

                does = {"aqkv": rotate_linear, "at": expand, "qkv": rotate_softmax, "sh": bias}
                does.update({k: rstd for k in LN_ORDER if k.startswith("ln_")})

                def run(i, steps):
                    for st in steps:
                        if st.kind in does:
                            does[st.kind](i, st)

                whole_program(pool, "gpsimd", run)


_INS = ["L0_attn_x", "L0_attn_Wq", "L0_attn_Wk", "L0_attn_Wv", "L0_attn_Wo", "L0_ffn_wqkv", "L0_ffn_q_scale",
        "L0_ffn_k_scale", "L0_ffn_wo", "L0_ffn_ln_g", "L0_ffn_ln_b", "L0_ffn_w1", "L0_ffn_b1", "L0_ffn_w2", "L0_ffn_b2"]


def kernel(**inputs):
    import concourse.bacc as bacc
    from concourse.bass_utils import run_bass_kernel_spmd

    nc = bacc.Bacc("TRN2", target_bir_lowering=False, num_devices=1)
    arrays = {f"in_{name}": np.ascontiguousarray(inputs[name]) for name in _INS}
    arrays["in_constants"] = CONSTANTS
    args = [nc.dram_tensor(n, a.shape, mybir.dt.from_np(a.dtype), kind="ExternalInput").ap() for n, a in arrays.items()]
    args.append(nc.dram_tensor("out_0", (B, T, D), mybir.dt.float32, kind="ExternalOutput").ap())
    build(nc, *args)
    r = run_bass_kernel_spmd(nc, [arrays], core_ids=[0])
    return r.results[0]["out_0"]
```
